# Optimizing a Trainium2 kernel written in Bass

```python
import numpy as np
import jax
import jax.numpy as jnp

def _softmax(x, axis=-1):
    return jax.nn.softmax(x, axis=axis)

def _gelu(x):
    return jax.nn.gelu(x, approximate=True)

def _silu(x):
    return jax.nn.silu(x)

def _sigmoid(x):
    return jax.nn.sigmoid(x)

def _layernorm(x, axis=-1, eps=1e-05):
    m = jnp.mean(x, axis=axis, keepdims=True)
    v = jnp.var(x, axis=axis, keepdims=True)
    return (x - m) / jnp.sqrt(v + eps)

def _scatter_add(tgt, idx, src, axis=0):
    return tgt.at[idx].add(src)

def _segment_sum(src, seg, n):
    return jax.ops.segment_sum(src, seg, n)
kernel_name = 'mk_gnn_resnorm_d1_gnn_r8_41c574'

def setup_inputs(seed: int=0):
    np.random.seed(seed)
    _w = jnp.asarray

    def _rec_inputs():
        import jax
        import jax.numpy as jnp
        _gk = jax.random.key(seed)
        x = -0.0003713 + 1 * jax.random.normal(jax.random.fold_in(_gk, 1), (6250, 128), jnp.float32)
        _s = jax.random.randint(jax.random.fold_in(_gk, 2), (50000,), 0, 6250, jnp.int32)
        _d = jax.random.randint(jax.random.fold_in(_gk, 3), (50000,), 0, 6250, jnp.int32)
        _loop = jnp.arange(6250, dtype=jnp.int32)
        src = jnp.concatenate([_s, _d, _loop])
        dst = jnp.concatenate([_d, _s, _loop])
        _o = jnp.argsort(dst, stable=True)
        src = src[_o]
        dst = dst[_o]
        edge_attr_128 = 9.41057e-06 + 1 * jax.random.normal(jax.random.fold_in(_gk, 12), (106250, 128), jnp.float32)
        return (x, src, dst, edge_attr_128)
    x, src, dst, edge_attr_128 = _rec_inputs()

    def _L0_gnn_setup():
        import jax, jax.numpy as jnp
        import numpy as np
        N_NODES = 12500
        N_EDGES = 200000
        D_NODE = 128
        D_EDGE = 128
        D_GLOB = 16
        D_HID = 256
        N_GRAPHS = 64
        key = jax.random.key(seed)
        ks = jax.random.split(key, 8)
        x = jax.random.normal(ks[0], (N_NODES, D_NODE), dtype=jnp.float32)
        edge_index = jax.random.randint(ks[1], (2, N_EDGES), 0, N_NODES, dtype=jnp.int64)
        edge_attr = jax.random.normal(ks[2], (N_EDGES, D_EDGE), dtype=jnp.float32)
        u = jax.random.normal(ks[3], (N_GRAPHS, D_GLOB), dtype=jnp.float32)
        batch = jnp.sort(jax.random.randint(ks[4], (N_NODES,), 0, N_GRAPHS, dtype=jnp.int64))
        d_in = D_NODE + D_EDGE + D_GLOB
        W1 = jax.random.normal(ks[5], (d_in, D_HID), dtype=jnp.float32) / np.sqrt(d_in)
        b1 = jnp.zeros((D_HID,), dtype=jnp.float32)
        W2 = jax.random.normal(ks[6], (D_HID, D_NODE), dtype=jnp.float32) / np.sqrt(D_HID)
        b2 = jnp.zeros((D_NODE,), dtype=jnp.float32)
        return {'x': x, 'edge_index': edge_index, 'edge_attr': edge_attr, 'u': u, 'batch': batch, 'W1': W1, 'b1': b1, 'W2': W2, 'b2': b2}
    _L0_gnn_all = _L0_gnn_setup()
    _L0_gnn_in = {k: v for k, v in _L0_gnn_all.items() if k in ('u', 'W1', 'b1', 'W2', 'b2')}
    del _L0_gnn_all
    return {'x': x, 'src': src, 'dst': dst, 'edge_attr_128': edge_attr_128, 'L0_gnn_u': _L0_gnn_in['u'], 'L0_gnn_W1': _L0_gnn_in['W1'], 'L0_gnn_b1': _L0_gnn_in['b1'], 'L0_gnn_W2': _L0_gnn_in['W2'], 'L0_gnn_b2': _L0_gnn_in['b2']}

def reference(x, src, dst, edge_attr_128, L0_gnn_u, L0_gnn_W1, L0_gnn_b1, L0_gnn_W2, L0_gnn_b2):
    import jax
    import jax.numpy as jnp

    def _L0_gnn_ref(x, edge_index, edge_attr, u, batch, W1, b1, W2, b2):
        import jax, jax.numpy as jnp
        import numpy as np
        N_NODES = 12500
        N_EDGES = 200000
        D_NODE = 128
        D_EDGE = 128
        D_GLOB = 16
        D_HID = 256
        N_GRAPHS = 64
        col = edge_index[1]
        agg = jax.ops.segment_sum(edge_attr, col, num_segments=x.shape[0])
        h = jnp.concatenate([x, agg, u[batch]], axis=1)
        h = jax.nn.relu(h @ W1 + b1)
        out = h @ W2 + b2
        return out + x
    edge_index = jnp.stack([src, dst])
    batch0 = jnp.zeros((6250,), jnp.int32)
    x = _layernorm(x + _L0_gnn_ref(x, edge_index, edge_attr_128, L0_gnn_u, batch0, L0_gnn_W1, L0_gnn_b1, L0_gnn_W2, L0_gnn_b2), axis=-1)
    return x

_drawn_inputs = setup_inputs


def setup_inputs(seed=0):
    import zlib

    import numpy as np

    out = dict(_drawn_inputs(seed))
    spreads = {'L0_gnn_b1': (0.0, 0.31), 'L0_gnn_b2': (0.0, 0.1)}
    factors = {}
    for name, (base, spread) in spreads.items():
        noise = np.random.default_rng([zlib.crc32(name.encode()), seed]).standard_normal(out[name].shape)
        drawn = base * np.exp(spread * noise) if base else spread * noise
        out[name] = jnp.asarray(drawn.astype(out[name].dtype))
    for name, factor in factors.items():
        out[name] = (out[name] * factor).astype(out[name].dtype)
    return out
```

```python
from contextlib import ExitStack

import concourse.bass as bass
from concourse import mybir

ALU = mybir.AluOpType
ACT = mybir.ActivationFunctionType
AX_X = mybir.AxisListType.X
F32 = mybir.dt.float32
I32 = mybir.dt.int32

P = 128
WIN = 64
R = 7
EDGES_WIN = R * P
WINDOWS_IT = 10
BANKS = 5
LEAD = 3
BLOCK = 512
J = BLOCK // P
SETTLED = 2
BASE_PITCH = 12
EPS = 1e-5
SET = 1
GEN_TILES = 10


def gnn_resnorm_kernel(nc: bass.Bass, x: bass.AP, dst: bass.AP, edges: bass.AP, u: bass.AP,
                       w1: bass.AP, b1: bass.AP, w2: bass.AP, b2: bass.AP, out: bass.AP):
    n_nodes, d = x.shape
    n_edges = edges.shape[0]
    d_glob = u.shape[1]
    hid = w1.shape[1]
    m_chunks = hid // P
    assert d == P and hid % P == 0 and w1.shape[0] == 2 * d + d_glob

    full_win = n_edges // EDGES_WIN
    rest_edges = n_edges - full_win * EDGES_WIN
    n_win = full_win + (rest_edges > 0)
    rest_rows, rest_tiles = divmod(rest_edges, R)
    iters = n_win // WINDOWS_IT
    tail_win = n_win - iters * WINDOWS_IT
    blocks = n_nodes // BLOCK
    rest_nodes = n_nodes - blocks * BLOCK
    agg_cols = (blocks + 1) * BLOCK
    assert n_win <= P and blocks == iters + 1 and 0 < rest_nodes <= P and rest_tiles > 0
    assert tail_win > 7 and agg_cols >= n_nodes - 1 + WIN
    last_block_from = iters * WINDOWS_IT + 7

    gen_steps = n_edges // (GEN_TILES * P)
    gen_rest = n_edges - gen_steps * GEN_TILES * P
    assert 0 < gen_rest <= P and GEN_TILES <= WINDOWS_IT * R

    with ExitStack() as ctx:
        def sb(name, shape, dt=F32):
            return ctx.enter_context(nc.sbuf_tensor(name, shape, dt))

        def psum(name, shape):
            return ctx.enter_context(nc.psum_tensor(name, shape, F32))

        def sem(name):
            return ctx.enter_context(nc.semaphore(name))

        edge_ring = sb("edge_ring", [P, WINDOWS_IT, R, d])
        onehot = sb("onehot", [P, BANKS, R, WIN])
        agg_t = sb("agg_t", [P, agg_cols])
        dst_rows = sb("dst_rows", [P, EDGES_WIN], I32)
        local_rows = sb("local_rows", [P, EDGES_WIN])
        local_t = sb("local_t", [P, n_win * R])
        base_row = sb("base_row", [1, iters * WINDOWS_IT + WINDOWS_IT], I32)
        bases = sb("bases", [1, (iters + 1) * BASE_PITCH], I32)
        base_f = sb("base_f", [P, 1])
        least_base = sb("least_base", [P, 1])
        late_base = sb("late_base", [P, 1])
        win_no = sb("win_no", [P, 1])
        viol = sb("viol", [P, 4])
        extreme = sb("extreme", [P, 2])
        worst = sb("worst", [P, 1])
        worst_row = sb("worst_row", [1, 1])
        flag = sb("flag", [1, 1], I32)
        iota = sb("iota", [P, BLOCK])
        ident = sb("ident", [P, P])
        w1_x = sb("w1_x", [P, hid])
        w1_a = sb("w1_a", [P, hid])
        w1_u = sb("w1_u", [d_glob, hid])
        u_col = sb("u_col", [d_glob, 1])
        b1_col = sb("b1_col", [P, m_chunks])
        bias = sb("bias", [P, m_chunks])
        w2_sb = sb("w2_sb", [P, m_chunks, d])
        b2_rows = sb("b2_rows", [P, d])
        half_b2 = sb("half_b2", [P, d])
        x_sb = sb("x_sb", [P, J, d])
        x_rest = sb("x_rest", [P, d])
        x_t = sb("x_t", [P, BLOCK])
        xb = sb("xb", [P, J, d])
        hid_t = sb("hid_t", [P, m_chunks, BLOCK])
        y = sb("y", [P, J, d])
        stats = sb("stats", [P, J, 6])
        mean_var = sb("mean_var", [P, J, 2])
        eps_col = sb("eps_col", [P, 1])
        std = sb("std", [P, J])
        rstd = sb("rstd", [P, J])
        shift = sb("shift", [P, J])
        z = sb("z", [P, J, d])
        gen_dst = sb("gen_dst", [P, GEN_TILES + 1], I32)
        gen_rel = sb("gen_rel", [P, GEN_TILES + 1])
        gen_onehot = sb("gen_onehot", [P, 2, BLOCK])

        win_sum = [psum(f"win_sum{i}", [P, BLOCK]) for i in range(BANKS)]
        xt_ps = psum("xt_ps", [P, BLOCK])
        hid_ps = psum("hid_ps", [P, BLOCK])
        out_ps = psum("out_ps", [P, BLOCK])

        pad_set = sem("pad_set")
        dst_landed = sem("dst_landed")
        bases_landed = sem("bases_landed")
        weights_landed = sem("weights_landed")
        edges_landed = [sem(f"edges_landed{i}") for i in range(WINDOWS_IT)]
        x_landed = sem("x_landed")
        rest_landed = sem("rest_landed")
        consts_ready = sem("consts_ready")
        agg_zeroed = sem("agg_zeroed")
        prep = sem("prep")
        local_ready = sem("local_ready")
        local_turned = sem("local_turned")
        local_t_ready = sem("local_t_ready")
        worst_ready = sem("worst_ready")
        worst_turned = sem("worst_turned")
        flag_ready = sem("flag_ready")
        bias_summed = sem("bias_summed")
        bias_ready = sem("bias_ready")
        half_b2_ready = sem("half_b2_ready")
        onehot_ready = sem("onehot_ready")
        window_summed = sem("window_summed")
        window_added = sem("window_added")
        x_turned = sem("x_turned")
        x_t_ready = sem("x_t_ready")
        hidden_summed = sem("hidden_summed")
        hidden_ready = sem("hidden_ready")
        out_summed = sem("out_summed")
        xb_ready = sem("xb_ready")
        y_ready = sem("y_ready")
        stats_ready = sem("stats_ready")
        moments_ready = sem("moments_ready")
        std_ready = sem("std_ready")
        rstd_ready = sem("rstd_ready")
        shift_ready = sem("shift_ready")
        normalized = sem("normalized")
        stored = sem("stored")
        gen_landed = sem("gen_landed")
        gen_rel_ready = sem("gen_rel_ready")
        gen_onehot_ready = sem("gen_onehot_ready")
        gen_tile_used = sem("gen_tile_used")
        gen_added = sem("gen_added")
        gen_zeroed = sem("gen_zeroed")

        PREP_BASES, PREP_BASE_F, PREP_LOCAL, PREP_MAX, PREP_MIN = 1, 2, 3, 4, 5

        def size(b):
            return (rest_nodes, 1) if b is REST else (P, J)

        REST = "rest"

        def no(b):
            return blocks if b is REST else b

        def window_edges(g):
            return edges[bass.ds(g * EDGES_WIN, EDGES_WIN), :].rearrange("(p r) f -> p (r f)", r=R)

        block = ctx.enter_context(nc.Block())

        @block.sync
        def _(sp):
            dst_full = dst[0:full_win * EDGES_WIN].rearrange("(w e) -> w e", e=EDGES_WIN)
            sp.dma_start(dst_rows[0:96, :], dst_full[0:96, :]).then_inc(dst_landed, 16)
            sp.wait_ge(pad_set, 1)
            sp.dma_start(dst_rows[96:full_win, :], dst_full[96:full_win, :]).then_inc(dst_landed, 16)
            sp.dma_start(dst_rows[full_win:n_win, 0:rest_edges],
                         dst[full_win * EDGES_WIN:n_edges].rearrange("(o e) -> o e", o=1)).then_inc(dst_landed, 16)

            def load_window(g, slot):
                sp.dma_start(edge_ring[:, slot].rearrange("p r f -> p (r f)"),
                             window_edges(g)).then_inc(edges_landed[slot], 16)

            def load_x(b):
                sp.wait_ge(x_turned, SET + b)
                sp.wait_ge(xb_ready, SET + b)
                sp.dma_start(x_sb[:].rearrange("p j f -> p (j f)"),
                             x[bass.ds(b * BLOCK, BLOCK), :].rearrange("(p j) f -> p (j f)", j=J)
                             ).then_inc(x_landed, 16)

            for i in range(WINDOWS_IT):
                load_window(i, i)

            sp.wait_ge(flag_ready, 1)
            general = sp.value_load(flag[0:1, 0:1], min_val=0, max_val=1)
            with sp.If(general > 0):
                sp.wait_ge(window_summed, WINDOWS_IT)
                step = GEN_TILES * P
                flat = edge_ring[:].rearrange("p s r f -> p (s r) f")
                at = gen_steps * step
                sp.dma_start(flat[0:gen_rest, GEN_TILES], edges[at:n_edges, :]).then_inc(gen_landed, 16)
                sp.dma_start(gen_dst[0:gen_rest, GEN_TILES:GEN_TILES + 1],
                             dst[at:n_edges].rearrange("(e o) -> e o", o=1)).then_inc(gen_landed, 16)
                with sp.Fori(0, gen_steps) as s:
                    sp.wait_ge(gen_tile_used, (blocks + 1) * (1 + GEN_TILES * s))
                    sp.dma_start(flat[:, 0:GEN_TILES].rearrange("p t f -> p (t f)"),
                                 edges[bass.ds(s * step, step), :].rearrange("(p t) f -> p (t f)", t=GEN_TILES)
                                 ).then_inc(gen_landed, 16)
                    sp.dma_start(gen_dst[:, 0:GEN_TILES],
                                 dst[bass.ds(s * step, step)].rearrange("(p t) -> p t", t=GEN_TILES)
                                 ).then_inc(gen_landed, 16)
                with sp.Fori(0, blocks) as b:
                    load_x(b)
            with sp.Else():
                with sp.Fori(1, iters) as k:
                    for i in range(WINDOWS_IT):
                        sp.wait_ge(window_summed, WINDOWS_IT * k + (i + 1 - WINDOWS_IT))
                        load_window(WINDOWS_IT * k + i, i)
                        if i == 1:
                            load_x(k - 1)
                for i in range(tail_win):
                    g = WINDOWS_IT * iters + i
                    sp.wait_ge(window_summed, g - WINDOWS_IT + 1)
                    if g < full_win:
                        load_window(g, i)
                    else:
                        src = edges[g * EDGES_WIN:g * EDGES_WIN + rest_rows * R, :].rearrange("(p r) f -> p (r f)", r=R)
                        dst_ap = edge_ring[0:rest_rows, i].rearrange("p r f -> p (r f)")
                        cut = rest_rows // 16 * 16
                        sp.dma_start(dst_ap[0:cut], src[0:cut]).then_inc(edges_landed[i], 16)
                        sp.dma_start(dst_ap[cut:rest_rows], src[cut:rest_rows]).then_inc(edges_landed[i], 16)
                        sp.dma_start(edge_ring[rest_rows:rest_rows + 1, i, 0:rest_tiles],
                                     edges[n_edges - rest_tiles:n_edges, :].rearrange("(o r) f -> o r f", o=1)
                                     ).then_inc(edges_landed[i], 16)
                    if i == 1:
                        load_x(iters - 1)
                load_x(iters)

        @block.gpsimd
        def _(pool):
            pool.sem_inc(xb_ready, SET)
            nc.gpsimd.iota(win_no[:], [[0, 1]], base=0, channel_multiplier=1,
                           allow_small_or_imprecise_dtypes=True)
            nc.gpsimd.iota(iota[:], [[1, BLOCK]], base=0, channel_multiplier=0,
                           allow_small_or_imprecise_dtypes=True).then_inc(consts_ready, 1)
            nc.gpsimd.memset(ident[:], 0.0).then_inc(consts_ready, 1)
            pool.wait_ge(consts_ready, 2)
            nc.gpsimd.affine_select(out=ident[:], in_=ident[:], compare_op=ALU.not_equal, fill=1.0, base=0,
                                    pattern=[[-1, P]], channel_multiplier=1).then_inc(consts_ready, 1)
            nc.gpsimd.memset(agg_t[:], 0.0).then_inc(agg_zeroed, 1)

            def add_half_b2(b):
                p, j = size(b)
                if b is REST:
                    pool.wait_ge(rest_landed, 32)
                else:
                    pool.wait_ge(x_landed, 16 * (b + 1))
                pool.wait_ge(y_ready, SET + no(b))
                src = x_rest[0:p, :].unsqueeze(1) if b is REST else x_sb[:]
                nc.gpsimd.tensor_tensor(xb[0:p, 0:j], src, half_b2[0:p, :].unsqueeze(1).broadcast_to([p, j, d]),
                                        ALU.add).then_inc(xb_ready, 1)

            pool.wait_ge(half_b2_ready, 1)
            with pool.Fori(0, blocks) as b:
                add_half_b2(b)
            add_half_b2(REST)

        @block.scalar
        def _(act):
            act.sem_inc(x_t_ready, SET)
            act.sem_inc(hidden_ready, SET)
            act.sem_inc(normalized, SET)
            act.sem_inc(stored, 16 * SET)
            loads = [
                (w1_x[:], w1[0:d, :]),
                (w1_a[:], w1[d:2 * d, :]),
                (w1_u[:], w1[2 * d:2 * d + d_glob, :]),
                (u_col[:], u[0:1, :].rearrange("o g -> g o")),
                (b1_col[:], b1.rearrange("(m p) -> p m", p=P)),
                (w2_sb[:], w2.rearrange("(m p) f -> p m f", p=P)),
                (b2_rows[:], b2.rearrange("(o f) -> o f", o=1).broadcast_to([P, d])),
            ]
            act.dma_start(base_row[0:1, 0:n_win],
                          dst.rearrange("(o e) -> o e", o=1)[:, 0:n_edges:EDGES_WIN],
                          allow_slow_non_contiguous=True).then_inc(bases_landed, 16)
            for to, src in loads:
                act.dma_start(to, src, allow_slow_non_contiguous=True).then_inc(weights_landed, 16)
            cut = rest_nodes // 16 * 16
            at = blocks * BLOCK
            act.dma_start(x_rest[0:cut, :], x[at:at + cut, :]).then_inc(rest_landed, 16)
            act.dma_start(x_rest[cut:rest_nodes, :], x[at + cut:n_nodes, :]).then_inc(rest_landed, 16)

            lt = local_t[:].rearrange("p (w r) -> p r w", r=R)
            act.wait_ge(local_turned, 1)
            nc.scalar.copy(lt[:, 0:4], xt_ps[:, 0:4 * n_win].rearrange("p (r w) -> p r w", r=4))
            act.wait_ge(local_turned, 2)
            nc.scalar.copy(lt[:, 4:R], hid_ps[:, 0:(R - 4) * n_win].rearrange("p (r w) -> p r w", r=R - 4)
                           ).then_inc(local_t_ready, 1)
            act.wait_ge(weights_landed, 16 * len(loads))
            nc.scalar.mul(half_b2[:], b2_rows[:], 0.5).then_inc(half_b2_ready, 1)
            act.wait_ge(bias_summed, 1)
            for m in range(m_chunks):
                last = nc.scalar.activation(bias[:, m:m + 1], out_ps[:, m:m + 1], ACT.Identity,
                                            bias=b1_col[:, m:m + 1])
            last.then_inc(bias_ready, 1)
            act.wait_ge(bias_ready, 1)

            def mlp_block(b):
                p, j = size(b)
                nodes = p * j
                n = no(b)
                act.wait_ge(x_turned, SET + n + 1)
                nc.scalar.copy(x_t[:, 0:nodes].rearrange("f (p j) -> f j p", j=j),
                               xt_ps[:, 0:nodes].rearrange("f (j p) -> f j p", j=j)).then_inc(x_t_ready, 1)
                for m in range(m_chunks):
                    act.wait_ge(hidden_summed, m_chunks * n + m + 1)
                    if m == 0:
                        act.wait_ge(out_summed, SET + n)
                    nc.scalar.activation(hid_t[:, m, 0:nodes].rearrange("h (j p) -> h j p", j=j),
                                         hid_ps[:, 0:nodes].rearrange("h (p j) -> h j p", j=j), ACT.Relu,
                                         bias=bias[:, m:m + 1]).then_inc(hidden_ready, 1)
                act.wait_ge(moments_ready, n + 1)
                nc.scalar.activation(std[0:p, 0:j], mean_var[0:p, 0:j, 1], ACT.Sqrt,
                                     bias=eps_col[0:p]).then_inc(std_ready, 1)
                act.wait_ge(shift_ready, n + 1)
                act.wait_ge(stored, 16 * (SET + n))
                for jj in range(j):
                    last = nc.scalar.activation(z[0:p, jj], y[0:p, jj], ACT.Identity, bias=shift[0:p, jj:jj + 1],
                                                scale=rstd[0:p, jj:jj + 1])
                last.then_inc(normalized, 1)
                act.wait_ge(normalized, SET + n + 1)

            with act.Fori(0, blocks) as b:
                mlp_block(b)
                act.dma_start(out[bass.ds(b * BLOCK, BLOCK), :].rearrange("(p j) f -> p (j f)", j=J),
                              z[:].rearrange("p j f -> p (j f)")).then_inc(stored, 16)
            mlp_block(REST)
            act.dma_start(out[at:at + cut, :], z[0:cut, 0]).then_inc(stored, 16)
            act.dma_start(out[at + cut:n_nodes, :], z[cut:rest_nodes, 0]).then_inc(stored, 16)
            act.wait_ge(stored, 16 * (SET + blocks + 2))

        @block.vector
        def _(dve):
            dve.sem_inc(y_ready, SET)
            nc.vector.memset(dst_rows[96:P, rest_edges:EDGES_WIN], n_nodes - 1).then_inc(pad_set, 1)
            nc.vector.memset(base_row[0:1, n_win:], 0)
            nc.vector.memset(eps_col[:], EPS).then_inc(pad_set, 1)
            dve.wait_ge(consts_ready, 1)
            nc.vector.tensor_scalar(least_base[:], win_no[:], BLOCK / WINDOWS_IT, -SETTLED * BLOCK / WINDOWS_IT,
                                    ALU.mult, ALU.add)
            nc.vector.tensor_scalar(late_base[:], win_no[:], last_block_from - 0.5, float(blocks * BLOCK),
                                    ALU.is_gt, ALU.mult).then_inc(pad_set, 1)
            dve.wait_ge(pad_set, 3)
            nc.vector.tensor_tensor(least_base[:], least_base[:], late_base[:], ALU.max).then_inc(pad_set, 1)
            dve.wait_ge(bases_landed, 16)
            nc.vector.tensor_scalar(bases[0:1, :].rearrange("o (k c) -> o k c", c=BASE_PITCH)[:, :, 0:WINDOWS_IT],
                                    base_row[0:1, :].rearrange("o (k c) -> o k c", c=WINDOWS_IT),
                                    float(n_nodes - 1), 0.0, ALU.min, ALU.max).then_inc(prep, 1)
            dve.wait_ge(dst_landed, 48)
            nc.vector.tensor_copy(base_f[0:n_win], dst_rows[0:n_win, 0:1]).then_inc(prep, 1)
            dve.wait_ge(prep, PREP_BASE_F)
            nc.vector.tensor_scalar(local_rows[0:n_win], dst_rows[0:n_win], base_f[0:n_win, 0:1], None,
                                    ALU.subtract).then_inc(prep, 1)
            dve.wait_ge(prep, PREP_LOCAL)

            def make_onehot(g, slot):
                loc = local_t[:, bass.ds(g * R, R)].unsqueeze(2).broadcast_to([P, R, WIN])
                cols = iota[:, 0:WIN].unsqueeze(1).broadcast_to([P, R, WIN])
                nc.vector.tensor_tensor(onehot[:, slot], cols, loc, ALU.is_equal).then_inc(onehot_ready, 1)

            def add_window(g, bank, base):
                dve.wait_ge(window_summed, g + 1)
                dve.wait_ge(window_added, g)
                at = agg_t[:, bass.ds(base, WIN)]
                nc.vector.tensor_tensor(at, at, win_sum[bank][:, 0:WIN], ALU.add).then_inc(window_added, 1)

            def load_bases(k, n):
                _, vals = nc.values_load_multi_w_load_instructions(
                    bases[0:1, bass.ds(k * BASE_PITCH, n)], engines=[mybir.EngineType.DVE],
                    min_val=0, max_val=n_nodes - 1, 
                    skip_runtime_bounds_check_because="bases were clamped to the nodes on the chip")
                return vals

            def block_step(b, step):
                p, j = size(b)
                n = no(b)
                if step == 0:
                    dve.wait_ge(out_summed, SET + n + 1)
                    dve.wait_ge(xb_ready, SET + n + 1)
                    dve.wait_ge(normalized, SET + n)
                    nc.vector.scalar_tensor_tensor(
                        out=y[0:p, 0:j].rearrange("p j f -> p (j f)"), in0=xb[0:p, 0:j].rearrange("p j f -> p (j f)"),
                        scalar=2.0, in1=out_ps[0:p, 0:j * d], op0=ALU.mult, op1=ALU.add).then_inc(y_ready, 1)
                elif step == 1:
                    dve.wait_ge(y_ready, SET + n + 1)
                    for jj in range(j):
                        last = nc.vector.bn_stats(stats[0:p, jj], y[0:p, jj])
                    last.then_inc(stats_ready, 1)
                elif step == 2:
                    dve.wait_ge(flag_ready, 1)
                    dve.wait_ge(stats_ready, n + 1)
                    for jj in range(j):
                        last = nc.vector.bn_aggr(mean_var[0:p, jj], stats[0:p, jj])
                    last.then_inc(moments_ready, 1)
                elif step == 3:
                    dve.wait_ge(std_ready, n + 1)
                    nc.vector.reciprocal(rstd[0:p, 0:j], std[0:p, 0:j]).then_inc(rstd_ready, 1)
                else:
                    dve.wait_ge(rstd_ready, n + 1)
                    nc.vector.scalar_tensor_tensor(out=shift[0:p, 0:j], in0=mean_var[0:p, 0:j, 0], scalar=-1.0,
                                                   in1=rstd[0:p, 0:j], op0=ALU.mult,
                                                   op1=ALU.mult).then_inc(shift_ready, 1)

            STEPS_AT = {5: (0,), 6: (1,), 7: (2,), 8: (3, 4)}

            def iteration(k, n, b):
                base = load_bases(k, n)
                for i in range(n):
                    if n == WINDOWS_IT or i + LEAD < n:
                        g = WINDOWS_IT * k + i + LEAD
                        dve.wait_ge(window_summed, g - BANKS + 1)
                        make_onehot(g, (i + LEAD) % BANKS)
                    if b is not None:
                        for step in STEPS_AT.get(i, ()):
                            block_step(b, step)
                    add_window(WINDOWS_IT * k + i, i % BANKS, base[i])

            dve.wait_ge(local_t_ready, 1)
            for g in range(LEAD):
                make_onehot(g, g)
            nc.vector.tensor_reduce(extreme[0:n_win, 0:1], local_rows[0:n_win], AX_X, ALU.max)
            nc.vector.tensor_reduce(extreme[0:n_win, 1:2], local_rows[0:n_win], AX_X, ALU.min).then_inc(prep, 1)
            dve.wait_ge(prep, 4)
            nc.vector.tensor_scalar(viol[0:n_win, 0:1], extreme[0:n_win, 0:1], float(WIN - 1), None, ALU.subtract)
            nc.vector.tensor_scalar(viol[0:n_win, 1:2], extreme[0:n_win, 1:2], -1.0, None, ALU.mult)
            nc.vector.tensor_tensor(viol[0:n_win, 2:3], least_base[0:n_win], base_f[0:n_win], ALU.subtract)
            nc.vector.tensor_scalar(viol[0:n_win, 3:4], base_f[0:n_win], float(n_nodes - 1), None,
                                    ALU.subtract).then_inc(prep, 1)
            dve.wait_ge(prep, 5)
            nc.vector.tensor_reduce(worst[0:n_win], viol[0:n_win], AX_X, ALU.max).then_inc(worst_ready, 1)
            dve.wait_ge(agg_zeroed, 1)
            base0 = load_bases(0, WINDOWS_IT)
            for i in range(WINDOWS_IT):
                g = i + LEAD
                if g >= BANKS:
                    dve.wait_ge(window_summed, g - BANKS + 1)
                make_onehot(g, g % BANKS)
                if i == 1:
                    dve.wait_ge(worst_turned, 1)
                    nc.vector.tensor_reduce(worst_row[0:1], out_ps[0:1, 256:256 + n_win], AX_X,
                                            ALU.max).then_inc(prep, 1)
                if i == 2:
                    dve.wait_ge(prep, 6)
                    nc.vector.tensor_scalar(flag[0:1], worst_row[0:1], 0.0, None, ALU.is_gt).then_inc(flag_ready, 1)
                add_window(i, i % BANKS, base0[i])

            dve.wait_ge(flag_ready, 1)
            general = dve.value_load(flag[0:1, 0:1], min_val=0, max_val=1)
            with dve.If(general > 0):
                dve.wait_ge(window_added, WINDOWS_IT)
                nc.vector.memset(agg_t[:], 0.0).then_inc(gen_zeroed, 1)
                dve.wait_ge(gen_zeroed, 1)

                def gen_match(tiles, rows, t0, rel_count, tiles_before, adds_before):
                    for t in range(tiles):
                        dve.wait_ge(gen_tile_used, tiles_before + t - 1)
                        nc.vector.tensor_scalar(gen_onehot[0:rows, t % 2], iota[0:rows], gen_rel[0:rows, t0 + t:t0 + t + 1],
                                                None, ALU.is_equal).then_inc(gen_onehot_ready, 1)
                    nc.vector.tensor_scalar(gen_rel[0:rows, t0:t0 + tiles], gen_rel[0:rows, t0:t0 + tiles],
                                            -float(BLOCK), None, ALU.add).then_inc(gen_rel_ready, 1)
                    dve.wait_ge(gen_rel_ready, rel_count)
                    dve.wait_ge(gen_tile_used, tiles_before + tiles)
                    dve.wait_ge(gen_added, adds_before)

                def gen_add(nb):
                    at = agg_t[:, bass.ds(nb * BLOCK, BLOCK)]
                    nc.vector.tensor_tensor(at, at, win_sum[0][:, :], ALU.add).then_inc(gen_added, 1)

                dve.wait_ge(gen_landed, 32)
                nc.vector.tensor_copy(gen_rel[0:gen_rest, GEN_TILES:], gen_dst[0:gen_rest, GEN_TILES:]
                                      ).then_inc(gen_rel_ready, 1)
                dve.wait_ge(gen_rel_ready, 1)
                for nb in range(blocks + 1):
                    nc.vector.tensor_scalar(gen_onehot[0:gen_rest, 0], iota[0:gen_rest],
                                            gen_rel[0:gen_rest, GEN_TILES:], None,
                                            ALU.is_equal).then_inc(gen_onehot_ready, 1)
                    nc.vector.tensor_scalar(gen_rel[0:gen_rest, GEN_TILES:], gen_rel[0:gen_rest, GEN_TILES:],
                                            -float(BLOCK), None, ALU.add).then_inc(gen_rel_ready, 1)
                    dve.wait_ge(gen_rel_ready, nb + 2)
                    dve.wait_ge(gen_tile_used, nb + 1)
                    gen_add(nb)
                nbs = blocks + 1
                with dve.Fori(0, gen_steps) as s:
                    dve.wait_ge(gen_landed, 32 * s + 64)
                    nc.vector.tensor_copy(gen_rel[:, 0:GEN_TILES], gen_dst[:, 0:GEN_TILES]).then_inc(gen_rel_ready, 1)
                    with dve.Fori(0, nbs) as nb:
                        n = nbs * s + nb
                        dve.wait_ge(gen_rel_ready, (nbs + 1) * (s + 1) + 1 + nb)
                        gen_match(GEN_TILES, P, 0, (nbs + 1) * (s + 1) + 2 + nb, nbs + GEN_TILES * n, nbs + n)
                        gen_add(nb)
                with dve.Fori(0, blocks) as b:
                    for step in range(5):
                        block_step(b, step)
                for step in range(5):
                    block_step(REST, step)
            with dve.Else():
                with dve.Fori(1, iters) as k:
                    iteration(k, WINDOWS_IT, k - 1)
                iteration(iters, tail_win, iters - 1)
                for b in (iters, REST):
                    for step in range(5):
                        block_step(b, step)

        @block.tensor
        def _(pe):
            pe.sem_inc(x_turned, SET)
            pe.sem_inc(out_summed, SET)
            pe.wait_ge(consts_ready, 3)
            pe.wait_ge(prep, PREP_LOCAL)
            for r in range(R):
                ps, col = (xt_ps, r) if r < 4 else (hid_ps, r - 4)
                last = nc.tensor.transpose(ps[:, col * n_win:(col + 1) * n_win],
                                           local_rows[0:n_win, r:EDGES_WIN:R], ident[0:n_win, 0:n_win])
                if r == 3 or r == R - 1:
                    last.then_inc(local_turned, 1)

            def sum_window(k, i, rows=None):
                g = WINDOWS_IT * k + i
                bank = i % BANKS
                pe.wait_ge(edges_landed[i], 16 * (k + 1) if rows is None else 16 * (k + 3))
                pe.wait_ge(onehot_ready, g + 1)
                if not isinstance(g, int) or g >= BANKS:
                    pe.wait_ge(window_added, g - BANKS + 1)
                for r in range(R):
                    p = P if rows is None else rows[r]
                    last = nc.tensor.matmul(win_sum[bank][:, 0:WIN], edge_ring[0:p, i, r], onehot[0:p, bank, r],
                                            start=(r == 0), stop=(r == R - 1))
                last.then_inc(window_summed, 1)

            def turn_x(b):
                p, j = size(b)
                n = no(b)
                if b is REST:
                    pe.wait_ge(rest_landed, 32)
                else:
                    pe.wait_ge(x_landed, 16 * (b + 1))
                pe.wait_ge(x_t_ready, SET + n)
                for jj in range(j):
                    src = x_rest[0:p, :] if b is REST else x_sb[:, jj]
                    last = nc.tensor.transpose(xt_ps[:, jj * p:(jj + 1) * p], src, ident[0:p, 0:p])
                last.then_inc(x_turned, 1)

            def sum_hidden(b, m):
                p, j = size(b)
                n = no(b)
                nodes = p * j
                pe.wait_ge(x_t_ready, SET + n + 1)
                pe.wait_ge(hidden_ready, SET + m_chunks * n + m)
                cols = slice(m * P, (m + 1) * P)
                nc.tensor.matmul(hid_ps[:, 0:nodes], w1_x[:, cols], x_t[:, 0:nodes], start=True, stop=False)
                nc.tensor.matmul(hid_ps[:, 0:nodes], w1_a[:, cols], agg_t[:, bass.ds(n * BLOCK, nodes)],
                                 start=False, stop=True).then_inc(hidden_summed, 1)

            def sum_out(b, js, last_part):
                p, j = size(b)
                n = no(b)
                pe.wait_ge(hidden_ready, SET + m_chunks * (n + 1))
                pe.wait_ge(y_ready, SET + n)
                for jj in js:
                    for m in range(m_chunks):
                        last = nc.tensor.matmul(out_ps[0:p, jj * d:(jj + 1) * d], hid_t[:, m, jj * p:(jj + 1) * p],
                                                w2_sb[:, m], start=(m == 0), stop=(m == m_chunks - 1))
                if last_part:
                    last.then_inc(out_summed, 1)

            for i in range(WINDOWS_IT):
                if i == 0:
                    pe.wait_ge(local_t_ready, 1)
                if i == 1:
                    pe.wait_ge(worst_ready, 1)
                    nc.tensor.transpose(out_ps[0:1, 256:256 + n_win], worst[0:n_win, 0:1],
                                        ident[0:n_win, 0:n_win]).then_inc(worst_turned, 1)
                if i == 4:
                    pe.wait_ge(flag_ready, 1)
                    pe.wait_ge(weights_landed, 16 * 7)
                    for m in range(m_chunks):
                        last = nc.tensor.matmul(out_ps[:, m:m + 1], w1_u[:, m * P:(m + 1) * P], u_col[:],
                                                start=True, stop=True)
                    last.then_inc(bias_summed, 1)
                sum_window(0, i)
            pe.wait_ge(bias_ready, 1)

            general = pe.value_load(flag[0:1, 0:1], min_val=0, max_val=1)
            with pe.If(general > 0):
                flat = edge_ring[:].rearrange("p s r f -> p (s r) f")
                nbs = blocks + 1
                pe.wait_ge(gen_zeroed, 1)
                pe.wait_ge(gen_landed, 32)
                for nb in range(nbs):
                    pe.wait_ge(gen_onehot_ready, nb + 1)
                    pe.wait_ge(gen_added, nb)
                    nc.tensor.matmul(win_sum[0][:, :], flat[0:gen_rest, GEN_TILES], gen_onehot[0:gen_rest, 0],
                                     start=True, stop=True).then_inc(gen_tile_used, 1)
                with pe.Fori(0, gen_steps) as s:
                    with pe.Fori(0, nbs) as nb:
                        n = nbs * s + nb
                        pe.wait_ge(gen_landed, 32 * s + 64)
                        pe.wait_ge(gen_added, nbs + n)
                        for t in range(GEN_TILES):
                            pe.wait_ge(gen_onehot_ready, nbs + GEN_TILES * n + (t + 1))
                            nc.tensor.matmul(win_sum[0][:, :], flat[:, t], gen_onehot[:, t % 2],
                                             start=(t == 0), stop=(t == GEN_TILES - 1)).then_inc(gen_tile_used, 1)
                pe.wait_ge(gen_added, nbs * (1 + gen_steps))
                with pe.Fori(0, blocks) as b:
                    turn_x(b)
                    for m in range(m_chunks):
                        sum_hidden(b, m)
                    sum_out(b, range(J), True)
                turn_x(REST)
                for m in range(m_chunks):
                    sum_hidden(REST, m)
                sum_out(REST, range(1), True)
            with pe.Else():
                with pe.Fori(1, iters) as k:
                    b = k - 1
                    for i in range(WINDOWS_IT):
                        if i == 0:
                            turn_x(b)
                        if i == 3:
                            pe.wait_ge(window_added, WINDOWS_IT * k + SETTLED)
                            sum_hidden(b, 0)
                        if i == 4:
                            sum_hidden(b, 1)
                        if i == 5:
                            sum_out(b, range(0, J), True)
                        sum_window(k, i)
                k, b = iters, iters - 1
                for i in range(tail_win):
                    if i == 0:
                        turn_x(b)
                    if i == 3:
                        pe.wait_ge(window_added, WINDOWS_IT * k + SETTLED)
                        sum_hidden(b, 0)
                    if i == 4:
                        sum_hidden(b, 1)
                    if i == 5:
                        sum_out(b, range(0, J), True)
                    if i == 6:
                        turn_x(iters)
                    if i == 8:
                        pe.wait_ge(window_added, last_block_from)
                        for m in range(m_chunks):
                            sum_hidden(iters, m)
                        turn_x(REST)
                    if i < tail_win - 1:
                        sum_window(k, i)
                sum_window(k, tail_win - 1, [rest_rows + (r < rest_tiles) for r in range(R)])
                sum_out(iters, range(J), True)
                pe.wait_ge(window_added, n_win)
                for m in range(m_chunks):
                    sum_hidden(REST, m)
                sum_out(REST, range(1), True)


_INS = ["x", "dst", "edge_attr_128", "L0_gnn_u", "L0_gnn_W1", "L0_gnn_b1", "L0_gnn_W2", "L0_gnn_b2"]


def kernel(**inputs):
    import numpy as _np
    import concourse.bacc as _bacc
    from concourse import mybir as _mybir
    from concourse.bass_utils import run_bass_kernel_spmd as _run

    nc = _bacc.Bacc("TRN2", target_bir_lowering=False, num_devices=1)
    arrays, args = {}, []
    for name in _INS:
        a = _np.ascontiguousarray(inputs[name])
        arrays[f"in_{name}_dram"] = a
        args.append(nc.dram_tensor(f"in_{name}_dram", a.shape, _mybir.dt.from_np(a.dtype), kind="ExternalInput").ap())
    shape = _np.shape(inputs["x"])
    args.append(nc.dram_tensor("out_0_dram", shape, _mybir.dt.float32, kind="ExternalOutput").ap())
    gnn_resnorm_kernel(nc, *args)
    r = _run(nc, [arrays], core_ids=[0])
    return r.results[0]["out_0_dram"]
```

```python
from contextlib import ExitStack

import concourse.bass as bass
from concourse import mybir

ALU = mybir.AluOpType
ACT = mybir.ActivationFunctionType
AX_X = mybir.AxisListType.X
F32 = mybir.dt.float32
I32 = mybir.dt.int32

P = 128
WIN = 32
R = 3
C = 4
TILES = C * R
SPAN = P
EDGES_WIN = R * P
EDGES_GRP = C * EDGES_WIN
IT = 6
ONEHOTS = 6
PLACES = 2
LEAD = 4
BASE_PITCH = 8
BLOCK = 512
J = BLOCK // P
EPS = 1e-5
SET = 1
GEN_TILES = 10


def gnn_resnorm_kernel(nc: bass.Bass, x: bass.AP, dst: bass.AP, edges: bass.AP, u: bass.AP,
                       w1: bass.AP, b1: bass.AP, w2: bass.AP, b2: bass.AP, out: bass.AP):
    n_nodes, d = x.shape
    n_edges = edges.shape[0]
    d_glob = u.shape[1]
    hid = w1.shape[1]
    m_chunks = hid // P
    assert d == P and hid % P == 0 and w1.shape[0] == 2 * d + d_glob

    full_grp = n_edges // EDGES_GRP
    rest_edges = n_edges - full_grp * EDGES_GRP
    n_grp = full_grp + 1
    rest_rows, rest_tiles = divmod(rest_edges, R)
    iters = n_grp // IT
    tail = n_grp - iters * IT
    blocks = n_nodes // BLOCK
    rest_nodes = n_nodes - blocks * BLOCK
    agg_cols = (blocks + 1) * BLOCK
    assert 0 < rest_edges <= EDGES_WIN and 0 < rest_nodes <= P and rest_tiles > 0
    assert n_grp <= P and agg_cols >= n_nodes - 1 + SPAN and blocks == iters + 1 and tail == 4

    half = BLOCK // 2
    full = iters - 1
    pieces = [(b * BLOCK, P, J) for b in range(full)]
    pieces += [(full * BLOCK + h * half, P, J // 2) for h in range(4)] + [(blocks * BLOCK, rest_nodes, 1)]
    A, B, C_, D, REST = range(full, full + 5)
    LAST = full - 1

    def piece(n):
        return pieces[n] if isinstance(n, int) else (n * BLOCK, P, J)

    def same(register_or_number, number):
        return isinstance(register_or_number, int) and register_or_number == number

    def second_half(n):
        return isinstance(n, int) and n in (B, D)

    def x_loads(n):
        return n + 1 if not isinstance(n, int) or n < A else (B + 1 if n <= B else D + 1)

    g0 = (iters - 1) * IT
    complete_at = {A: g0, B: g0 + 3, C_: g0 + 6, D: g0 + 9, REST: n_grp}

    late_groups = [(complete_at[n], pieces[n][0] + half) for n in (A, B, C_, D)]

    gen_steps = n_edges // (GEN_TILES * P)
    gen_rest = n_edges - gen_steps * GEN_TILES * P
    assert 0 < gen_rest <= P and GEN_TILES < IT * TILES

    with ExitStack() as ctx:
        def sb(name, shape, dt=F32):
            return ctx.enter_context(nc.sbuf_tensor(name, shape, dt))

        def psum(name, shape):
            return ctx.enter_context(nc.psum_tensor(name, shape, F32))

        def sem(name):
            return ctx.enter_context(nc.semaphore(name))

        edge_ring = sb("edge_ring", [P, IT, TILES, d])
        onehot = sb("onehot", [P, ONEHOTS, TILES, WIN])
        sums = sb("sums", [P, 2, d])
        agg_t = sb("agg_t", [P, agg_cols])
        dst_rows = sb("dst_rows", [P, C, EDGES_WIN], I32)
        local_rows = sb("local_rows", [P, C, EDGES_WIN])
        local_t = sb("local_t", [P, n_grp * TILES])
        base_row = sb("base_row", [1, (iters + 1) * IT], I32)
        bases = sb("bases", [1, (iters + 1) * BASE_PITCH], I32)
        rel = sb("rel", [P, C])
        rel_t = sb("rel_t", [C, P])
        win_row = sb("win_row", [C, 1])
        rel_cols = sb("rel_cols", [P, n_grp])
        to_window = sb("to_window", [C, P])
        place = sb("place", [P, PLACES, SPAN])
        base_f = sb("base_f", [P, C])
        least_base = sb("least_base", [P, 1])
        late_base = sb("late_base", [P, len(late_groups)])
        row_no = sb("row_no", [P, 1])
        viol = sb("viol", [P, 6, C])
        extreme = sb("extreme", [P, 2, C])
        worst = sb("worst", [P, 1])
        worst_row = sb("worst_row", [1, 1])
        flag = sb("flag", [1, 1], I32)
        iota = sb("iota", [P, BLOCK])
        ident = sb("ident", [P, P])
        w1_x = sb("w1_x", [P, hid])
        w1_a = sb("w1_a", [P, hid])
        w1_u = sb("w1_u", [d_glob, hid])
        u_col = sb("u_col", [d_glob, 1])
        b1_col = sb("b1_col", [P, m_chunks])
        bias = sb("bias", [P, m_chunks])
        w2_sb = sb("w2_sb", [P, m_chunks, d])
        b2_rows = sb("b2_rows", [P, d])
        half_b2 = sb("half_b2", [P, d])
        x_sb = sb("x_sb", [P, J, d])
        x_rest = sb("x_rest", [P, d])
        x_t = sb("x_t", [P, BLOCK])
        xb = sb("xb", [P, J, d])
        hid_t = sb("hid_t", [P, m_chunks, BLOCK])
        y = sb("y", [P, J, d])
        stats = sb("stats", [P, J, 6])
        mean_var = sb("mean_var", [P, J, 2])
        eps_col = sb("eps_col", [P, 1])
        std = sb("std", [P, J])
        rstd = sb("rstd", [P, J])
        z = sb("z", [P, J, d])
        gen_dst = sb("gen_dst", [P, GEN_TILES + 1], I32)
        gen_rel = sb("gen_rel", [P, GEN_TILES + 1])
        gen_onehot = sb("gen_onehot", [P, 2, BLOCK])

        sum_ps = [psum(f"sum_ps{i}", [P, BLOCK]) for i in range(2)]
        turn_ps = [psum(f"turn_ps{i}", [P, BLOCK]) for i in range(2)]
        xt_ps = psum("xt_ps", [P, BLOCK])
        hid_ps = [psum(f"hid_ps{m}", [P, BLOCK]) for m in range(m_chunks)]
        out_ps = psum("out_ps", [P, BLOCK])

        pad_set = sem("pad_set")
        dst_landed = sem("dst_landed")
        bases_landed = sem("bases_landed")
        weights_landed = sem("weights_landed")
        edges_landed = [sem(f"edges_landed{i}") for i in range(IT)]
        x_landed = sem("x_landed")
        rest_landed = sem("rest_landed")
        consts_ready = sem("consts_ready")
        pool_step = sem("pool_step")
        agg_zeroed = sem("agg_zeroed")
        prep = sem("prep")
        local_ready = sem("local_ready")
        local_turned = sem("local_turned")
        local_t_ready = sem("local_t_ready")
        worst_ready = sem("worst_ready")
        worst_turned = sem("worst_turned")
        flag_ready = sem("flag_ready")
        bias_summed = sem("bias_summed")
        bias_ready = sem("bias_ready")
        half_b2_ready = sem("half_b2_ready")
        onehot_ready = sem("onehot_ready")
        group_summed = sem("group_summed")
        group_copied = sem("group_copied")
        group_turned = sem("group_turned")
        group_added = sem("group_added")
        rel_ready = sem("rel_ready")
        rel_turned = sem("rel_turned")
        rel_t_ready = sem("rel_t_ready")
        rel_spread = sem("rel_spread")
        rel_cols_ready = sem("rel_cols_ready")
        place_ready = sem("place_ready")
        x_turned = sem("x_turned")
        x_t_ready = sem("x_t_ready")
        hidden_summed = sem("hidden_summed")
        hidden_ready = sem("hidden_ready")
        out_summed = sem("out_summed")
        xb_ready = sem("xb_ready")
        y_ready = sem("y_ready")
        stats_ready = sem("stats_ready")
        moments_ready = sem("moments_ready")
        std_ready = sem("std_ready")
        rstd_ready = sem("rstd_ready")
        normalized = sem("normalized")
        stored = sem("stored")
        gen_landed = sem("gen_landed")
        gen_rel_ready = sem("gen_rel_ready")
        gen_onehot_ready = sem("gen_onehot_ready")
        gen_tile_used = sem("gen_tile_used")
        gen_added = sem("gen_added")
        gen_zeroed = sem("gen_zeroed")

        PREP_BASE_F, PREP_LOCAL = 2, 3
        per_bank = BLOCK // n_grp
        turned_to = [xt_ps, hid_ps[0]]
        assert per_bank * len(turned_to) >= TILES

        block = ctx.enter_context(nc.Block())

        @block.sync
        def _(sp):
            dst_full = dst[0:full_grp * EDGES_GRP].rearrange("(g c e) -> g c e", c=C, e=EDGES_WIN)
            sp.dma_start(dst_rows[0:64], dst_full[0:64]).then_inc(dst_landed, 16)
            sp.wait_ge(pad_set, 1)
            sp.dma_start(dst_rows[64:full_grp], dst_full[64:full_grp]).then_inc(dst_landed, 16)
            sp.dma_start(dst_rows[full_grp:n_grp, 0, 0:rest_edges],
                         dst[full_grp * EDGES_GRP:n_edges].rearrange("(o e) -> o e", o=1)).then_inc(dst_landed, 16)

            def load_group(g, slot):
                sp.dma_start(edge_ring[:, slot].rearrange("p (c r) f -> p c (r f)", c=C),
                             edges[bass.ds(g * EDGES_GRP, EDGES_GRP), :].rearrange("(c p r) f -> p c (r f)", c=C, p=P)
                             ).then_inc(edges_landed[slot], 16)

            def load_x(n, at=0):
                node0, p, j = piece(n)
                sp.dma_start(x_sb[:, at:at + j].rearrange("p j f -> p (j f)"),
                             x[bass.ds(node0, p * j), :].rearrange("(p j) f -> p (j f)", j=j)
                             ).then_inc(x_landed, 16)

            def x_sb_free(n):
                sp.wait_ge(x_turned, SET + n)
                sp.wait_ge(xb_ready, SET + n)

            def load_x_halves(n):
                x_sb_free(n)
                load_x(n, 0)
                load_x(n + 1, J // 2)

            for i in range(IT):
                load_group(i, i)

            sp.wait_ge(flag_ready, 1)
            general = sp.value_load(flag[0:1, 0:1], min_val=0, max_val=1)
            with sp.If(general > 0):
                sp.wait_ge(group_summed, IT)
                step = GEN_TILES * P
                flat = edge_ring[:].rearrange("p s r f -> p (s r) f")
                at = gen_steps * step
                sp.dma_start(flat[0:gen_rest, GEN_TILES], edges[at:n_edges, :]).then_inc(gen_landed, 16)
                sp.dma_start(gen_dst[0:gen_rest, GEN_TILES:GEN_TILES + 1],
                             dst[at:n_edges].rearrange("(e o) -> e o", o=1)).then_inc(gen_landed, 16)
                with sp.Fori(0, gen_steps) as s:
                    sp.wait_ge(gen_tile_used, (blocks + 1) * (1 + GEN_TILES * s))
                    sp.dma_start(flat[:, 0:GEN_TILES].rearrange("p t f -> p (t f)"),
                                 edges[bass.ds(s * step, step), :].rearrange("(p t) f -> p (t f)", t=GEN_TILES)
                                 ).then_inc(gen_landed, 16)
                    sp.dma_start(gen_dst[:, 0:GEN_TILES],
                                 dst[bass.ds(s * step, step)].rearrange("(p t) -> p t", t=GEN_TILES)
                                 ).then_inc(gen_landed, 16)
                with sp.Fori(0, full) as n:
                    x_sb_free(n)
                    load_x(n)
                load_x_halves(A)
                load_x_halves(C_)
            with sp.Else():
                with sp.Fori(1, iters) as k:
                    for i in range(IT):
                        sp.wait_ge(group_summed, IT * k + (i + 1 - IT))
                        load_group(IT * k + i, i)
                        if i == 1:
                            x_sb_free(k - 1)
                            load_x(k - 1)
                for i in range(tail):
                    g = IT * iters + i
                    sp.wait_ge(group_summed, g - IT + 1)
                    if g < full_grp:
                        load_group(g, i)
                    else:
                        src = edges[g * EDGES_GRP:g * EDGES_GRP + rest_rows * R, :].rearrange("(p r) f -> p (r f)", r=R)
                        to = edge_ring[0:rest_rows, i, 0:R].rearrange("p r f -> p (r f)")
                        cut = rest_rows // 16 * 16
                        sp.dma_start(to[0:cut], src[0:cut]).then_inc(edges_landed[i], 16)
                        if cut < rest_rows:
                            sp.dma_start(to[cut:rest_rows], src[cut:rest_rows]).then_inc(edges_landed[i], 16)
                        sp.dma_start(edge_ring[rest_rows:rest_rows + 1, i, 0:rest_tiles],
                                     edges[n_edges - rest_tiles:n_edges, :].rearrange("(o r) f -> o r f", o=1)
                                     ).then_inc(edges_landed[i], 16)
                    if i == 1:
                        load_x_halves(A)
                load_x_halves(C_)

        @block.gpsimd
        def _(pool):
            pool.sem_inc(xb_ready, SET)
            nc.gpsimd.iota(row_no[:], [[0, 1]], base=0, channel_multiplier=1,
                           allow_small_or_imprecise_dtypes=True)
            nc.gpsimd.iota(win_row[:], [[0, 1]], base=0, channel_multiplier=WIN,
                           allow_small_or_imprecise_dtypes=True)
            nc.gpsimd.iota(iota[:], [[1, BLOCK]], base=0, channel_multiplier=0,
                           allow_small_or_imprecise_dtypes=True).then_inc(consts_ready, 1)
            nc.gpsimd.memset(ident[:], 0.0).then_inc(consts_ready, 1)
            pool.wait_ge(consts_ready, 2)
            nc.gpsimd.affine_select(out=ident[:], in_=ident[:], compare_op=ALU.not_equal, fill=1.0, base=0,
                                    pattern=[[-1, P]], channel_multiplier=1).then_inc(consts_ready, 1)
            nc.gpsimd.memset(to_window[:], 1.0).then_inc(pool_step, 1)
            pool.wait_ge(pool_step, 1)
            nc.gpsimd.affine_select(out=to_window[:], in_=to_window[:], compare_op=ALU.is_ge, fill=0.0, base=0,
                                    pattern=[[1, P]], channel_multiplier=-WIN).then_inc(pool_step, 1)
            pool.wait_ge(pool_step, 2)
            nc.gpsimd.affine_select(out=to_window[:], in_=to_window[:], compare_op=ALU.is_ge, fill=0.0,
                                    base=WIN - 1, pattern=[[-1, P]], channel_multiplier=WIN).then_inc(consts_ready, 1)
            nc.gpsimd.memset(agg_t[:], 0.0).then_inc(agg_zeroed, 1)

            def add_half_b2(n):
                _, p, j = piece(n)
                if same(n, REST):
                    pool.wait_ge(rest_landed, 32)
                    src = x_rest[0:p, :].unsqueeze(1)
                else:
                    pool.wait_ge(x_landed, 16 * x_loads(n))
                    src = x_sb[:, j:2 * j] if second_half(n) else x_sb[:, 0:j]
                pool.wait_ge(y_ready, SET + n)
                nc.gpsimd.tensor_tensor(xb[0:p, 0:j], src, half_b2[0:p, :].unsqueeze(1).broadcast_to([p, j, d]),
                                        ALU.add).then_inc(xb_ready, 1)

            pool.wait_ge(half_b2_ready, 1)
            with pool.Fori(0, full) as n:
                add_half_b2(n)
            for n in range(full, len(pieces)):
                add_half_b2(n)

        @block.scalar
        def _(act):
            nc.scalar.preload_act_table(ACT.Sqrt)
            act.sem_inc(x_t_ready, SET)
            act.sem_inc(hidden_ready, SET)
            act.sem_inc(stored, 16 * SET)
            loads = [
                (w1_x[:], w1[0:d, :]),
                (w1_a[:], w1[d:2 * d, :]),
                (w1_u[:], w1[2 * d:2 * d + d_glob, :]),
                (u_col[:], u[0:1, :].rearrange("o g -> g o")),
                (b1_col[:], b1.rearrange("(m p) -> p m", p=P)),
                (w2_sb[:], w2.rearrange("(m p) f -> p m f", p=P)),
                (b2_rows[:], b2.rearrange("(o f) -> o f", o=1).broadcast_to([P, d])),
            ]
            act.dma_start(base_row[0:1, 1:n_grp + 1],
                          dst.rearrange("(o e) -> o e", o=1)[:, 0:n_edges:EDGES_GRP],
                          allow_slow_non_contiguous=True).then_inc(bases_landed, 16)
            for to, src in loads:
                act.dma_start(to, src, allow_slow_non_contiguous=True).then_inc(weights_landed, 16)
            cut = rest_nodes // 16 * 16
            at = blocks * BLOCK
            act.dma_start(x_rest[0:cut, :], x[at:at + cut, :]).then_inc(rest_landed, 16)
            act.dma_start(x_rest[cut:rest_nodes, :], x[at + cut:n_nodes, :]).then_inc(rest_landed, 16)

            lt = local_t[:].rearrange("p (g t) -> p t g", t=TILES)
            t0 = 0
            for n, ps in enumerate(turned_to):
                act.wait_ge(local_turned, n + 1)
                t1 = min(t0 + per_bank, TILES)
                last = nc.scalar.copy(lt[:, t0:t1], ps[:, 0:(t1 - t0) * n_grp].rearrange("p (t g) -> p t g", g=n_grp))
                t0 = t1
            last.then_inc(local_t_ready, 1)
            act.wait_ge(weights_landed, 16 * len(loads))
            nc.scalar.mul(half_b2[:], b2_rows[:], 0.5).then_inc(half_b2_ready, 1)
            def copy_group(g, i):
                act.wait_ge(group_summed, g + 1)
                if not isinstance(g, int) or g >= 2:
                    act.wait_ge(group_turned, g - 1)
                w = C * WIN if not same(g, full_grp) else WIN
                nc.scalar.copy(sums[0:w, i % 2], sum_ps[i % 2][0:w, 0:d]).then_inc(group_copied, 1)

            def copy_x_t(n):
                _, p, j = piece(n)
                act.wait_ge(x_turned, SET + n + 1)
                nc.scalar.copy(x_t[:, 0:p * j].rearrange("f (p j) -> f j p", j=j),
                               xt_ps[:, 0:p * j].rearrange("f (j p) -> f j p", j=j)).then_inc(x_t_ready, 1)

            def relu(n, m):
                _, p, j = piece(n)
                act.wait_ge(hidden_summed, m_chunks * n + m + 1)
                if m == 0:
                    act.wait_ge(out_summed, SET + n)
                nc.scalar.activation(hid_t[:, m, 0:p * j].rearrange("h (j p) -> h j p", j=j),
                                     hid_ps[m][:, 0:p * j].rearrange("h (p j) -> h j p", j=j), ACT.Relu,
                                     bias=bias[:, m:m + 1]).then_inc(hidden_ready, 1)

            def root(n):
                _, p, j = piece(n)
                act.wait_ge(moments_ready, n + 1)
                nc.scalar.activation(std[0:p, 0:j], mean_var[0:p, 0:j, 1], ACT.Sqrt,
                                     bias=eps_col[0:p]).then_inc(std_ready, 1)

            def store(n):
                node0, p, j = piece(n)
                act.wait_ge(normalized, SET + n + 1)
                if same(n, REST):
                    act.dma_start(out[at:at + cut, :], z[0:cut, 0]).then_inc(stored, 16)
                    act.dma_start(out[at + cut:n_nodes, :], z[cut:rest_nodes, 0]).then_inc(stored, 16)
                else:
                    act.dma_start(out[bass.ds(node0, p * j), :].rearrange("(p j) f -> p (j f)", j=j),
                                  z[:, 0:j].rearrange("p j f -> p (j f)")).then_inc(stored, 16)

            for g in range(IT):
                copy_group(g, g)
                if g == 3:
                    act.wait_ge(bias_summed, 1)
                    for m in range(m_chunks):
                        last = nc.scalar.activation(bias[:, m:m + 1], out_ps[:, m:m + 1], ACT.Identity,
                                                    bias=b1_col[:, m:m + 1])
                    last.then_inc(bias_ready, 1)
            act.wait_ge(bias_ready, 1)
            act.wait_ge(flag_ready, 1)
            general = act.value_load(flag[0:1, 0:1], min_val=0, max_val=1)
            with act.If(general > 0):
                def mlp(n):
                    copy_x_t(n)
                    for m in range(m_chunks):
                        relu(n, m)
                    root(n)
                    store(n)

                with act.Fori(0, full) as n:
                    mlp(n)
                for n in range(full, len(pieces)):
                    mlp(n)
            with act.Else():
                def relus(n):
                    for m in range(m_chunks):
                        relu(n, m)

                def iteration(k, before=True):
                    n, g = k - 1, IT * k
                    copy_group(g, 0)
                    if before:
                        root(n - 1)
                    copy_x_t(n)
                    copy_group(g + 1, 1)
                    relu(n, 0)
                    if before:
                        store(n - 1)
                    copy_group(g + 2, 2)
                    relu(n, 1)
                    for i in range(3, IT):
                        copy_group(g + i, i)
                        if same(k, iters - 1) and i == 3:
                            copy_x_t(A)
                        if same(k, iters - 1) and i == 4:
                            relus(A)

                iteration(1, False)
                with act.Fori(2, iters - 1) as k:
                    iteration(k)
                iteration(iters - 1)
                g = IT * iters
                copy_x_t(B)
                root(LAST)
                copy_group(g, 0)
                relus(B)
                store(LAST)
                root(A)
                copy_x_t(C_)
                copy_group(g + 1, 1)
                relus(C_)
                store(A)
                root(B)
                copy_x_t(D)
                copy_group(g + 2, 2)
                copy_group(full_grp, 3)
                relus(D)
                copy_x_t(REST)
                root(C_)
                store(B)
                relus(REST)
                store(C_)
                for n in (D, REST):
                    root(n)
                    store(n)
            act.wait_ge(stored, 16 * (SET + REST + 2))

        @block.vector
        def _(dve):
            dve.sem_inc(y_ready, SET)
            dve.sem_inc(normalized, SET)
            nc.vector.memset(dst_rows[64:P, 0, rest_edges:], n_nodes - 1)
            nc.vector.memset(dst_rows[64:P, 1:C], n_nodes - 1).then_inc(pad_set, 1)
            nc.vector.memset(base_row[0:1, 0:1], 0)
            nc.vector.memset(base_row[0:1, n_grp + 1:], 0)
            nc.vector.memset(eps_col[:], EPS).then_inc(pad_set, 1)
            dve.wait_ge(consts_ready, 1)
            nc.vector.tensor_scalar(least_base[:], row_no[:], BLOCK / IT, None, ALU.mult)
            for n, (g, least) in enumerate(late_groups):
                last = nc.vector.tensor_scalar(late_base[:, n:n + 1], row_no[:], g - 0.5, float(least),
                                               ALU.is_gt, ALU.mult)
            last.then_inc(pad_set, 1)
            dve.wait_ge(pad_set, 3)
            for n in range(len(late_groups)):
                nc.vector.tensor_tensor(least_base[:], least_base[:], late_base[:, n:n + 1],
                                        ALU.max).then_inc(pad_set, 1)
                dve.wait_ge(pad_set, 4 + n)
            dve.wait_ge(bases_landed, 16)
            nc.vector.tensor_scalar(bases[0:1, :].rearrange("o (k i) -> o k i", i=BASE_PITCH)[:, :, 0:IT],
                                    base_row[0:1, :].rearrange("o (k i) -> o k i", i=IT),
                                    float(n_nodes - 1), 0.0, ALU.min, ALU.max).then_inc(prep, 1)
            dve.wait_ge(dst_landed, 48)
            nc.vector.tensor_copy(base_f[0:n_grp], dst_rows[0:n_grp, :, 0]).then_inc(prep, 1)
            dve.wait_ge(prep, PREP_BASE_F)
            nc.vector.tensor_scalar(rel[0:n_grp], base_f[0:n_grp], base_f[0:n_grp, 0:1], None,
                                    ALU.subtract).then_inc(rel_ready, 1)
            nc.vector.tensor_tensor(local_rows[0:n_grp], dst_rows[0:n_grp],
                                    base_f[0:n_grp].unsqueeze(2).broadcast_to([n_grp, C, EDGES_WIN]),
                                    ALU.subtract).then_inc(prep, 1)
            dve.wait_ge(rel_turned, 1)
            nc.vector.tensor_scalar(rel_t[:, 0:n_grp], out_ps[0:C, 0:n_grp], win_row[:], None,
                                    ALU.subtract).then_inc(rel_t_ready, 1)
            dve.wait_ge(rel_spread, 1)
            nc.vector.tensor_scalar(rel_cols[:], out_ps[:, 128:128 + n_grp], row_no[:], None,
                                    ALU.add).then_inc(rel_cols_ready, 1)
            dve.wait_ge(prep, PREP_LOCAL)

            def make_onehot(g, slot):
                loc = local_t[:, bass.ds(g * TILES, TILES)].unsqueeze(2).broadcast_to([P, TILES, WIN])
                cols = iota[:, 0:WIN].unsqueeze(1).broadcast_to([P, TILES, WIN])
                nc.vector.tensor_tensor(onehot[:, slot], cols, loc, ALU.is_equal).then_inc(onehot_ready, 1)

            def next_onehot(g, i):
                if not isinstance(g, int) or g + LEAD >= ONEHOTS:
                    dve.wait_ge(group_summed, g + LEAD - ONEHOTS + 1)
                make_onehot(g + LEAD, (i + LEAD) % ONEHOTS)

            def load_bases(k, n=IT):
                _, vals = nc.values_load_multi_w_load_instructions(
                    bases[0:1, bass.ds(k * BASE_PITCH, n)], engines=[mybir.EngineType.DVE],
                    min_val=0, max_val=n_nodes - 1,
                    skip_runtime_bounds_check_because="bases were clamped to the nodes on the chip")
                return vals

            def make_place(g, i):
                nc.vector.tensor_scalar(place[:, i % PLACES], iota[:, 0:SPAN], rel_cols[:, bass.ds(g, 1)], None,
                                        ALU.is_equal).then_inc(place_ready, 1)

            def add_group(g, i, base):
                dve.wait_ge(group_turned, g + 1)
                dve.wait_ge(group_added, g)
                to = agg_t[:, bass.ds(base, SPAN)]
                nc.vector.tensor_tensor(to, to, turn_ps[i % 2][:, 0:SPAN], ALU.add).then_inc(group_added, 1)

            def norm_step(n, step):
                _, p, j = piece(n)
                if step == 0:
                    dve.wait_ge(out_summed, SET + n + 1)
                    dve.wait_ge(xb_ready, SET + n + 1)
                    dve.wait_ge(normalized, SET + n)
                    nc.vector.scalar_tensor_tensor(
                        out=y[0:p, 0:j].rearrange("p j f -> p (j f)"), in0=xb[0:p, 0:j].rearrange("p j f -> p (j f)"),
                        scalar=2.0, in1=out_ps[0:p, 0:j * d], op0=ALU.mult, op1=ALU.add).then_inc(y_ready, 1)
                elif step == 1:
                    dve.wait_ge(y_ready, SET + n + 1)
                    for jj in range(j):
                        last = nc.vector.bn_stats(stats[0:p, jj], y[0:p, jj])
                    last.then_inc(stats_ready, 1)
                elif step == 2:
                    dve.wait_ge(flag_ready, 1)
                    dve.wait_ge(stats_ready, n + 1)
                    for jj in range(j):
                        last = nc.vector.bn_aggr(mean_var[0:p, jj], stats[0:p, jj])
                    last.then_inc(moments_ready, 1)
                elif step == 3:
                    dve.wait_ge(std_ready, n + 1)
                    nc.vector.reciprocal(rstd[0:p, 0:j], std[0:p, 0:j]).then_inc(rstd_ready, 1)
                elif step == 4:
                    dve.wait_ge(rstd_ready, n + 1)
                    dve.wait_ge(stored, 16 * (SET + n))
                    for jj in range(j):
                        last = nc.vector.tensor_scalar(z[0:p, jj], y[0:p, jj], mean_var[0:p, jj, 0:1],
                                                       rstd[0:p, jj:jj + 1], ALU.subtract, ALU.mult)
                    last.then_inc(normalized, 1)

            def moments(n):
                for step in range(3):
                    norm_step(n, step)

            def normalize(n):
                for step in (3, 4):
                    norm_step(n, step)

            dve.wait_ge(local_t_ready, 1)
            for g in range(LEAD):
                make_onehot(g, g)
            nc.vector.tensor_reduce(extreme[0:n_grp, 0], local_rows[0:n_grp], AX_X, ALU.max)
            nc.vector.tensor_reduce(extreme[0:n_grp, 1], local_rows[0:n_grp], AX_X, ALU.min).then_inc(prep, 1)
            dve.wait_ge(prep, 4)
            nc.vector.tensor_scalar(viol[0:n_grp, 0], extreme[0:n_grp, 0], float(WIN - 1), None, ALU.subtract)
            nc.vector.tensor_scalar(viol[0:n_grp, 1], extreme[0:n_grp, 1], -1.0, None, ALU.mult)
            nc.vector.tensor_scalar(viol[0:n_grp, 2], base_f[0:n_grp], -1.0, least_base[0:n_grp], ALU.mult, ALU.add)
            nc.vector.tensor_scalar(viol[0:n_grp, 3], base_f[0:n_grp], float(n_nodes - 1), None,
                                    ALU.subtract)
            nc.vector.tensor_scalar(viol[0:n_grp, 4], rel[0:n_grp], float(SPAN - WIN), None, ALU.subtract)
            nc.vector.tensor_scalar(viol[0:n_grp, 5], rel[0:n_grp], -1.0, None, ALU.mult).then_inc(prep, 1)
            dve.wait_ge(prep, 5)
            nc.vector.tensor_reduce(worst[0:n_grp], viol[0:n_grp].rearrange("g v c -> g (v c)"), AX_X,
                                    ALU.max).then_inc(worst_ready, 1)
            dve.wait_ge(rel_cols_ready, 1)
            dve.wait_ge(agg_zeroed, 1)
            base0 = load_bases(0)
            for g in range(IT):
                next_onehot(g, g)
                if g == 1:
                    dve.wait_ge(worst_turned, 1)
                    nc.vector.tensor_reduce(worst_row[0:1], out_ps[0:1, 256:256 + n_grp], AX_X,
                                            ALU.max).then_inc(prep, 1)
                    dve.wait_ge(prep, 6)
                    nc.vector.tensor_scalar(flag[0:1], worst_row[0:1], 0.0, None, ALU.is_gt).then_inc(flag_ready, 1)
                make_place(g, g)
                if g > 0:
                    add_group(g - 1, g - 1, base0[g])


            dve.wait_ge(flag_ready, 1)
            general = dve.value_load(flag[0:1, 0:1], min_val=0, max_val=1)
            with dve.If(general > 0):
                dve.wait_ge(group_added, IT - 1)
                nc.vector.memset(agg_t[:], 0.0).then_inc(gen_zeroed, 1)
                dve.wait_ge(gen_zeroed, 1)

                def gen_match(tiles, rows, t0, rel_count, tiles_before, adds_before):
                    for t in range(tiles):
                        dve.wait_ge(gen_tile_used, tiles_before + t - 1)
                        nc.vector.tensor_scalar(gen_onehot[0:rows, t % 2], iota[0:rows], gen_rel[0:rows, t0 + t:t0 + t + 1],
                                                None, ALU.is_equal).then_inc(gen_onehot_ready, 1)
                    dve.wait_ge(gen_tile_used, tiles_before + tiles)
                    nc.vector.tensor_scalar(gen_rel[0:rows, t0:t0 + tiles], gen_rel[0:rows, t0:t0 + tiles],
                                            -float(BLOCK), None, ALU.add).then_inc(gen_rel_ready, 1)
                    dve.wait_ge(gen_rel_ready, rel_count)
                    dve.wait_ge(gen_added, adds_before)

                def gen_add(nb):
                    at = agg_t[:, bass.ds(nb * BLOCK, BLOCK)]
                    nc.vector.tensor_tensor(at, at, sum_ps[0][:, :], ALU.add).then_inc(gen_added, 1)

                dve.wait_ge(gen_landed, 32)
                nc.vector.tensor_copy(gen_rel[0:gen_rest, GEN_TILES:], gen_dst[0:gen_rest, GEN_TILES:]
                                      ).then_inc(gen_rel_ready, 1)
                dve.wait_ge(gen_rel_ready, 1)
                for nb in range(blocks + 1):
                    nc.vector.tensor_scalar(gen_onehot[0:gen_rest, 0], iota[0:gen_rest],
                                            gen_rel[0:gen_rest, GEN_TILES:], None,
                                            ALU.is_equal).then_inc(gen_onehot_ready, 1)
                    dve.wait_ge(gen_tile_used, nb + 1)
                    nc.vector.tensor_scalar(gen_rel[0:gen_rest, GEN_TILES:], gen_rel[0:gen_rest, GEN_TILES:],
                                            -float(BLOCK), None, ALU.add).then_inc(gen_rel_ready, 1)
                    dve.wait_ge(gen_rel_ready, nb + 2)
                    gen_add(nb)
                nbs = blocks + 1
                with dve.Fori(0, gen_steps) as s:
                    dve.wait_ge(gen_landed, 32 * s + 64)
                    nc.vector.tensor_copy(gen_rel[:, 0:GEN_TILES], gen_dst[:, 0:GEN_TILES]).then_inc(gen_rel_ready, 1)
                    with dve.Fori(0, nbs) as nb:
                        n = nbs * s + nb
                        dve.wait_ge(gen_rel_ready, (nbs + 1) * (s + 1) + 1 + nb)
                        gen_match(GEN_TILES, P, 0, (nbs + 1) * (s + 1) + 2 + nb, nbs + GEN_TILES * n, nbs + n)
                        gen_add(nb)
                with dve.Fori(0, full) as n:
                    moments(n)
                    normalize(n)
                for n in range(full, len(pieces)):
                    moments(n)
                    normalize(n)
            with dve.Else():
                def group(g, i, bases_before):
                    if not isinstance(g, int) or g + LEAD < n_grp:
                        next_onehot(g, i)
                    make_place(g, i)
                    add_group(g - 1, (i - 1) % IT, bases_before[i])

                def iteration(k, before=True):
                    base = load_bases(k)
                    for i in range(IT):
                        group(IT * k + i, i, base)
                        if i == 1 and before:
                            normalize(k - 2)
                        if i == 4:
                            moments(k - 1)

                iteration(1, False)
                with dve.Fori(2, iters) as k:
                    iteration(k)
                g = IT * iters
                base = load_bases(iters, tail + 1)
                group(g, 0, base)
                normalize(LAST)
                moments(A)
                group(g + 1, 1, base)
                normalize(A)
                moments(B)
                group(g + 2, 2, base)
                normalize(B)
                moments(C_)
                group(full_grp, 3, base)
                add_group(full_grp, 3, base[tail])
                normalize(C_)
                for n in (D, REST):
                    moments(n)
                    normalize(n)

        @block.tensor
        def _(pe):
            pe.sem_inc(x_turned, SET)
            pe.sem_inc(out_summed, SET)
            pe.wait_ge(consts_ready, 4)
            pe.wait_ge(rel_ready, 1)
            nc.tensor.transpose(out_ps[0:C, 0:n_grp], rel[0:n_grp, :], ident[0:n_grp, 0:n_grp]).then_inc(rel_turned, 1)
            pe.wait_ge(rel_t_ready, 1)
            nc.tensor.matmul(out_ps[:, 128:128 + n_grp], to_window[:], rel_t[:, 0:n_grp], start=True,
                             stop=True).then_inc(rel_spread, 1)
            pe.wait_ge(prep, PREP_LOCAL)
            for t in range(TILES):
                c, r = divmod(t, R)
                ps, col = turned_to[t // per_bank], t % per_bank
                last = nc.tensor.transpose(ps[:, col * n_grp:(col + 1) * n_grp], local_rows[0:n_grp, c, r::R],
                                           ident[0:n_grp, 0:n_grp])
                if col == per_bank - 1 or t == TILES - 1:
                    last.then_inc(local_turned, 1)

            def sum_group(g, i, rounds):
                pe.wait_ge(edges_landed[i], 16 * rounds)
                pe.wait_ge(onehot_ready, g + 1)
                if not isinstance(g, int) or g >= 2:
                    pe.wait_ge(group_copied, g - 1)
                for r in range(R):
                    for c in range(C if not same(g, full_grp) else 1):
                        p = P if not same(g, full_grp) else rest_rows + (r < rest_tiles)
                        last = nc.tensor.matmul(sum_ps[i % 2][c * WIN:(c + 1) * WIN, 0:d],
                                                onehot[0:p, i % ONEHOTS, c * R + r], edge_ring[0:p, i, c * R + r],
                                                start=(r == 0), stop=(r == R - 1))
                last.then_inc(group_summed, 1)

            def turn_group(g, i):
                pe.wait_ge(group_copied, g + 1)
                pe.wait_ge(place_ready, g + 1)
                if not isinstance(g, int) or g >= 2:
                    pe.wait_ge(group_added, g - 1)
                w = C * WIN if not same(g, full_grp) else WIN
                nc.tensor.matmul(turn_ps[i % 2][:, 0:SPAN], sums[0:w, i % 2], place[0:w, i % PLACES],
                                 start=True, stop=True).then_inc(group_turned, 1)

            def turn_x(n):
                _, p, j = piece(n)
                if same(n, REST):
                    pe.wait_ge(rest_landed, 32)
                else:
                    pe.wait_ge(x_landed, 16 * x_loads(n))
                pe.wait_ge(x_t_ready, SET + n)
                for jj in range(j):
                    src = x_rest[0:p, :] if same(n, REST) else x_sb[:, jj + (j if second_half(n) else 0)]
                    last = nc.tensor.transpose(xt_ps[:, jj * p:(jj + 1) * p], src, ident[0:p, 0:p])
                last.then_inc(x_turned, 1)

            def sum_hidden(n, m):
                node0, p, j = piece(n)
                nodes = p * j
                pe.wait_ge(x_t_ready, SET + n + 1)
                pe.wait_ge(hidden_ready, SET + m_chunks * n + (m - 1))
                cols = slice(m * P, (m + 1) * P)
                nc.tensor.matmul(hid_ps[m][:, 0:nodes], w1_x[:, cols], x_t[:, 0:nodes], start=True, stop=False)
                nc.tensor.matmul(hid_ps[m][:, 0:nodes], w1_a[:, cols], agg_t[:, bass.ds(node0, nodes)],
                                 start=False, stop=True).then_inc(hidden_summed, 1)

            def sum_out(n):
                _, p, j = piece(n)
                pe.wait_ge(hidden_ready, SET + m_chunks * (n + 1))
                pe.wait_ge(y_ready, SET + n)
                for jj in range(j):
                    for m in range(m_chunks):
                        last = nc.tensor.matmul(out_ps[0:p, jj * d:(jj + 1) * d], hid_t[:, m, jj * p:(jj + 1) * p],
                                                w2_sb[:, m], start=(m == 0), stop=(m == m_chunks - 1))
                last.then_inc(out_summed, 1)

            pe.wait_ge(local_t_ready, 1)
            for g in range(IT):
                sum_group(g, g, 1)
                if g == 0:
                    pe.wait_ge(worst_ready, 1)
                    nc.tensor.transpose(out_ps[0:1, 256:256 + n_grp], worst[0:n_grp, 0:1],
                                        ident[0:n_grp, 0:n_grp]).then_inc(worst_turned, 1)
                if g > 0:
                    turn_group(g - 1, g - 1)
                if g == 3:
                    pe.wait_ge(flag_ready, 1)
                    pe.wait_ge(weights_landed, 16 * 7)
                    for m in range(m_chunks):
                        last = nc.tensor.matmul(out_ps[:, m:m + 1], w1_u[:, m * P:(m + 1) * P], u_col[:],
                                                start=True, stop=True)
                    last.then_inc(bias_summed, 1)
            pe.wait_ge(bias_ready, 1)

            general = pe.value_load(flag[0:1, 0:1], min_val=0, max_val=1)
            with pe.If(general > 0):
                flat = edge_ring[:].rearrange("p s r f -> p (s r) f")
                nbs = blocks + 1
                pe.wait_ge(group_copied, IT)
                pe.wait_ge(gen_zeroed, 1)
                pe.wait_ge(gen_landed, 32)
                for nb in range(nbs):
                    pe.wait_ge(gen_onehot_ready, nb + 1)
                    pe.wait_ge(gen_added, nb)
                    nc.tensor.matmul(sum_ps[0][:, :], flat[0:gen_rest, GEN_TILES], gen_onehot[0:gen_rest, 0],
                                     start=True, stop=True).then_inc(gen_tile_used, 1)
                with pe.Fori(0, gen_steps) as s:
                    with pe.Fori(0, nbs) as nb:
                        n = nbs * s + nb
                        pe.wait_ge(gen_landed, 32 * s + 64)
                        pe.wait_ge(gen_added, nbs + n)
                        for t in range(GEN_TILES):
                            pe.wait_ge(gen_onehot_ready, nbs + GEN_TILES * n + (t + 1))
                            nc.tensor.matmul(sum_ps[0][:, :], flat[:, t], gen_onehot[:, t % 2],
                                             start=(t == 0), stop=(t == GEN_TILES - 1)).then_inc(gen_tile_used, 1)
                pe.wait_ge(gen_added, nbs * (1 + gen_steps))
                def mlp(n):
                    turn_x(n)
                    for m in range(m_chunks):
                        sum_hidden(n, m)
                    sum_out(n)

                with pe.Fori(0, full) as n:
                    mlp(n)
                for n in range(full, len(pieces)):
                    mlp(n)
            with pe.Else():
                def group(g, i, rounds):
                    sum_group(g, i, rounds)
                    turn_group(g - 1, (i - 1) % IT)

                def hidden(n):
                    pe.wait_ge(group_added, complete_at[n])
                    for m in range(m_chunks):
                        sum_hidden(n, m)

                def iteration(k):
                    n, g = k - 1, IT * k
                    for i in range(IT):
                        group(g + i, i, k + 1)
                        if i == 0:
                            turn_x(n)
                        if i == 1:
                            pe.wait_ge(group_added, g)
                            sum_hidden(n, 0)
                        if i == 2:
                            sum_hidden(n, 1)
                        if i == 3:
                            sum_out(n)
                        if same(k, iters - 1):
                            if i == 3:
                                turn_x(A)
                            if i == 4:
                                hidden(A)
                            if i == 5:
                                sum_out(A)
                                turn_x(B)

                with pe.Fori(1, iters - 1) as k:
                    iteration(k)
                iteration(iters - 1)
                g, rounds = IT * iters, iters + 1
                group(g, 0, rounds)
                hidden(B)
                sum_out(B)
                turn_x(C_)
                group(g + 1, 1, rounds)
                hidden(C_)
                sum_out(C_)
                turn_x(D)
                group(g + 2, 2, rounds)
                group(full_grp, 3, iters + 2 + (rest_rows % 16 > 0))
                turn_x(REST)
                turn_group(full_grp, 3)
                hidden(D)
                sum_out(D)
                hidden(REST)
                sum_out(REST)


_INS = ["x", "dst", "edge_attr_128", "L0_gnn_u", "L0_gnn_W1", "L0_gnn_b1", "L0_gnn_W2", "L0_gnn_b2"]


def kernel(**inputs):
    import numpy as _np
    import concourse.bacc as _bacc
    from concourse import mybir as _mybir
    from concourse.bass_utils import run_bass_kernel_spmd as _run

    nc = _bacc.Bacc("TRN2", target_bir_lowering=False, num_devices=1)
    arrays, args = {}, []
    for name in _INS:
        a = _np.ascontiguousarray(inputs[name])
        arrays[f"in_{name}_dram"] = a
        args.append(nc.dram_tensor(f"in_{name}_dram", a.shape, _mybir.dt.from_np(a.dtype), kind="ExternalInput").ap())
    shape = _np.shape(inputs["x"])
    args.append(nc.dram_tensor("out_0_dram", shape, _mybir.dt.float32, kind="ExternalOutput").ap())
    gnn_resnorm_kernel(nc, *args)
    r = _run(nc, [arrays], core_ids=[0])
    return r.results[0]["out_0_dram"]
```

```python
from contextlib import ExitStack

import concourse.bass as bass
from concourse import mybir

ALU = mybir.AluOpType
ACT = mybir.ActivationFunctionType
AX_X = mybir.AxisListType.X
F32 = mybir.dt.float32
I32 = mybir.dt.int32

P = 128
WIN = 32
R = 3
C = 4
TILES = C * R
SPAN = P
EDGES_WIN = R * P
EDGES_GRP = C * EDGES_WIN
IT = 6
ONEHOTS = 6
PLACES = 3
EARLY = 2
LEAD = 4
BASE_PITCH = 8
BLOCK = 512
J = BLOCK // P
EPS = 1e-5
SET = 1
GEN_TILES = 10


def gnn_resnorm_kernel(nc: bass.Bass, x: bass.AP, dst: bass.AP, edges: bass.AP, u: bass.AP,
                       w1: bass.AP, b1: bass.AP, w2: bass.AP, b2: bass.AP, out: bass.AP):
    n_nodes, d = x.shape
    n_edges = edges.shape[0]
    d_glob = u.shape[1]
    hid = w1.shape[1]
    m_chunks = hid // P
    assert d == P and hid % P == 0 and w1.shape[0] == 2 * d + d_glob

    full_grp = n_edges // EDGES_GRP
    rest_edges = n_edges - full_grp * EDGES_GRP
    n_grp = full_grp + 1
    rest_rows, rest_tiles = divmod(rest_edges, R)
    iters = n_grp // IT
    tail = n_grp - iters * IT
    blocks = n_nodes // BLOCK
    agg_cols = (blocks + 1) * BLOCK
    assert 0 < rest_edges <= EDGES_WIN and rest_tiles > 0
    assert n_grp <= P and agg_cols >= n_nodes - 1 + SPAN and blocks == iters + 1 and tail == 4

    full = iters - 1
    late0 = full * BLOCK
    half = BLOCK // 2
    rest0 = late0 + 3 * half + 2 * P
    rest_nodes = n_nodes - rest0
    assert 0 < rest_nodes <= P
    pieces = [(b * BLOCK, P, J) for b in range(full)]
    pieces += [(late0 + h * half, P, J // 2) for h in range(3)]
    pieces += [(rest0 - 2 * P, P, 1), (rest0 - P, P, 1), (rest0, rest_nodes, 1)]
    A, B, C_, D, E, REST = late = range(full, full + 6)
    LAST = full - 1
    late_slot = {A: 0, B: 2, C_: 4, D: 6, E: 7, REST: 8}
    late_slots = 9
    pool_z = (LAST, A, B, C_)
    rest_cut = rest_nodes // 16 * 16

    x_steps = iters - 3
    x_cols = (rest0 - late0) // x_steps
    assert x_steps * x_cols == rest0 - late0

    def piece(n):
        return pieces[n] if isinstance(n, int) else (n * BLOCK, P, J)

    def same(register_or_number, number):
        return isinstance(register_or_number, int) and register_or_number == number

    def is_late(n):
        return isinstance(n, int) and n >= full

    g0 = (iters - 1) * IT
    complete_at = {A: g0, B: g0 + 3, C_: g0 + 6, D: g0 + 7, E: g0 + 9, REST: n_grp}

    LAST_COMPLETE = g0 - 2

    late_groups = [(LAST_COMPLETE, late0)] + [(complete_at[n], pieces[n + 1][0]) for n in (A, B, C_, D, E)]

    gen_steps = n_edges // (GEN_TILES * P)
    gen_rest = n_edges - gen_steps * GEN_TILES * P
    assert 0 < gen_rest <= P and GEN_TILES < IT * TILES

    with ExitStack() as ctx:
        def sb(name, shape, dt=F32):
            return ctx.enter_context(nc.sbuf_tensor(name, shape, dt))

        def psum(name, shape):
            return ctx.enter_context(nc.psum_tensor(name, shape, F32))

        def sem(name):
            return ctx.enter_context(nc.semaphore(name))

        edge_ring = sb("edge_ring", [P, IT, TILES, d])
        onehot = sb("onehot", [P, ONEHOTS, TILES, WIN])
        sums = sb("sums", [P, 2, d])
        agg_t = sb("agg_t", [P, agg_cols])
        dst_rows = sb("dst_rows", [P, C, EDGES_WIN], I32)
        local_rows = sb("local_rows", [P, C, EDGES_WIN])
        local_t = sb("local_t", [P, n_grp * TILES])
        base_row = sb("base_row", [1, (iters + 1) * IT], I32)
        bases = sb("bases", [1, (iters + 1) * BASE_PITCH], I32)
        rel = sb("rel", [P, C])
        rel_t = sb("rel_t", [C, P])
        win_row = sb("win_row", [C, 1])
        rel_cols = sb("rel_cols", [P, n_grp])
        to_window = sb("to_window", [C, P])
        place = sb("place", [P, PLACES, SPAN])
        base_f = sb("base_f", [P, C])
        least_base = sb("least_base", [P, 1])
        late_base = sb("late_base", [P, len(late_groups)])
        row_no = sb("row_no", [P, 1])
        viol = sb("viol", [P, 6, C])
        extreme = sb("extreme", [P, 2, C])
        worst = sb("worst", [P, 1])
        worst_row = sb("worst_row", [1, 1])
        flag = sb("flag", [1, 1], I32)
        iota = sb("iota", [P, BLOCK])
        ident = sb("ident", [P, P])
        w1_x = sb("w1_x", [P, hid])
        w1_a = sb("w1_a", [P, hid])
        w1_u = sb("w1_u", [d_glob, hid])
        u_col = sb("u_col", [d_glob, 1])
        b1_col = sb("b1_col", [P, m_chunks])
        bias = sb("bias", [P, m_chunks])
        w2_sb = sb("w2_sb", [P, m_chunks, d])
        b2_rows = sb("b2_rows", [P, d])
        half_b2 = sb("half_b2", [P, d])
        x_sb = sb("x_sb", [P, J, d])
        x_t = sb("x_t", [P, BLOCK])
        xb = sb("xb", [P, J, d])
        hid_t = sb("hid_t", [P, m_chunks, BLOCK])
        y = sb("y", [P, J, d])
        stats = sb("stats", [P, J, 6])
        mean_var = sb("mean_var", [P, J, 2])
        eps_col = sb("eps_col", [P, 1])
        std = sb("std", [P, J])
        rstd = sb("rstd", [P, J])
        z = sb("z", [P, full * J, d])
        x_late = sb("x_late", [P, late_slots, d])
        x_t_late = sb("x_t_late", [P, n_nodes - late0])
        x_hid_late = sb("x_hid_late", [P, m_chunks, x_steps * x_cols])
        xb_late = sb("xb_late", [P, late_slots, d])
        hid_t_late = sb("hid_t_late", [P, m_chunks, n_nodes - late0])
        y_late = sb("y_late", [P, late_slots, d])
        stats_late = sb("stats_late", [P, late_slots, 6])
        mean_var_late = sb("mean_var_late", [P, late_slots, 2])
        std_late = sb("std_late", [P, late_slots])
        rstd_late = sb("rstd_late", [P, late_slots])
        z_late = sb("z_late", [P, late_slots, d])
        gen_dst = sb("gen_dst", [P, GEN_TILES + 1], I32)
        gen_rel = sb("gen_rel", [P, GEN_TILES + 1])
        gen_onehot = sb("gen_onehot", [P, 2, BLOCK])

        sum_ps = [psum(f"sum_ps{i}", [P, BLOCK]) for i in range(2)]
        turn_ps = [psum(f"turn_ps{i}", [P, BLOCK]) for i in range(2)]
        xt_ps = psum("xt_ps", [P, BLOCK])
        hid_ps = [psum(f"hid_ps{m}", [P, BLOCK]) for m in range(m_chunks)]
        out_ps = psum("out_ps", [P, BLOCK])

        def rows(n, buffer, late_buffer):
            _, p, j = piece(n)
            return late_buffer[0:p, late_slot[n]:late_slot[n] + j] if is_late(n) else buffer[0:p]

        def z_rows(n):
            return rows(n, z, z_late) if is_late(n) else z[:, bass.ds(n * J, J)]

        def late_bank(n):
            _, p, j = pieces[n]
            return hid_ps[(n - full) % 2][:, 0:m_chunks * half].rearrange("h (m c) -> h m c", m=m_chunks)[:, :, 0:p * j]

        rest_banks = [ps[:, BLOCK - rest_nodes:] for ps in sum_ps]

        def out_bank(n):
            return xt_ps if is_late(n) and (n - full) % 2 == 0 else out_ps

        pad_set = sem("pad_set")
        dst_landed = sem("dst_landed")
        bases_landed = sem("bases_landed")
        weights_landed = sem("weights_landed")
        edges_landed = [sem(f"edges_landed{i}") for i in range(IT)]
        x_landed = sem("x_landed")
        x_late_landed = sem("x_late_landed")
        x_late_turned = sem("x_late_turned")
        x_t_late_ready = sem("x_t_late_ready")
        xb_late_ready = sem("xb_late_ready")
        consts_ready = sem("consts_ready")
        pool_step = sem("pool_step")
        agg_zeroed = sem("agg_zeroed")
        prep = sem("prep")
        local_turned = sem("local_turned")
        local_t_ready = sem("local_t_ready")
        worst_ready = sem("worst_ready")
        worst_turned = sem("worst_turned")
        flag_ready = sem("flag_ready")
        bias_summed = sem("bias_summed")
        bias_ready = sem("bias_ready")
        half_b2_ready = sem("half_b2_ready")
        onehot_ready = sem("onehot_ready")
        group_summed = sem("group_summed")
        group_copied = sem("group_copied")
        group_turned = sem("group_turned")
        group_added = sem("group_added")
        rel_ready = sem("rel_ready")
        rel_turned = sem("rel_turned")
        rel_t_ready = sem("rel_t_ready")
        rel_spread = sem("rel_spread")
        rel_cols_ready = sem("rel_cols_ready")
        place_ready = sem("place_ready")
        x_turned = sem("x_turned")
        x_t_ready = sem("x_t_ready")
        hidden_summed = sem("hidden_summed")
        hidden_ready = sem("hidden_ready")
        late_x_summed = sem("late_x_summed")
        late_x_ready = sem("late_x_ready")
        late_x_added = sem("late_x_added")
        out_summed = sem("out_summed")
        xb_ready = sem("xb_ready")
        y_ready = sem("y_ready")
        stats_ready = sem("stats_ready")
        moments_ready = sem("moments_ready")
        std_ready = sem("std_ready")
        rstd_ready = sem("rstd_ready")
        normalized = sem("normalized")
        stored = sem("stored")
        end_normalized = sem("end_normalized")
        gen_landed = sem("gen_landed")
        gen_rel_ready = sem("gen_rel_ready")
        gen_onehot_ready = sem("gen_onehot_ready")
        gen_tile_used = sem("gen_tile_used")
        gen_added = sem("gen_added")
        gen_zeroed = sem("gen_zeroed")

        PREP_BASE_F, PREP_LOCAL, PREP_EXTREME, PREP_VIOL, PREP_WORST_ROW = 2, 3, 4, 5, 6
        rel_at, spread_at, worst_at = (slice(n * P, n * P + n_grp) for n in range(3))
        n_weights = 7
        per_bank = BLOCK // n_grp
        turned_to = [xt_ps, hid_ps[0]]
        assert per_bank * len(turned_to) >= TILES

        block = ctx.enter_context(nc.Block())

        @block.sync
        def _(sp):
            dst_full = dst[0:full_grp * EDGES_GRP].rearrange("(g c e) -> g c e", c=C, e=EDGES_WIN)
            sp.dma_start(dst_rows[0:64], dst_full[0:64]).then_inc(dst_landed, 16)
            sp.dma_start(x_late[:, 0:late_slot[D]].rearrange("p (n j) f -> p n (j f)", j=J // 2),
                         x[late0:rest0 - 2 * P, :].rearrange("(n p j) f -> p n (j f)", p=P, j=J // 2)
                         ).then_inc(x_late_landed, 16)
            sp.wait_ge(pad_set, 1)
            sp.dma_start(dst_rows[64:full_grp], dst_full[64:full_grp]).then_inc(dst_landed, 16)
            sp.dma_start(dst_rows[full_grp:n_grp, 0, 0:rest_edges],
                         dst[full_grp * EDGES_GRP:n_edges].rearrange("(o e) -> o e", o=1)).then_inc(dst_landed, 16)

            def load_group(g, slot):
                sp.dma_start(edge_ring[:, slot].rearrange("p (c r) f -> p c (r f)", c=C),
                             edges[bass.ds(g * EDGES_GRP, EDGES_GRP), :].rearrange("(c p r) f -> p c (r f)", c=C, p=P)
                             ).then_inc(edges_landed[slot], 16)

            def load_x(n):
                sp.wait_ge(x_turned, SET + n)
                sp.wait_ge(xb_ready, SET + n)
                sp.dma_start(x_sb[:].rearrange("p j f -> p (j f)"),
                             x[bass.ds(n * BLOCK, BLOCK), :].rearrange("(p j) f -> p (j f)", j=J)
                             ).then_inc(x_landed, 16)

            def store():
                sp.wait_ge(normalized, SET + LAST)
                sp.dma_start(out[0:LAST * BLOCK, :].rearrange("(n p j) f -> p n (j f)", p=P, j=J),
                             z[:, 0:LAST * J].rearrange("p (n j) f -> p n (j f)", j=J)).then_inc(stored, 16)
                for n in (LAST, *late):
                    node0, p, j = pieces[n]
                    if n in pool_z:
                        sp.wait_ge(normalized, SET + n + 1)
                    else:
                        sp.wait_ge(end_normalized, n - C_)
                    cut = p if p == P else rest_cut
                    src = z_rows(n).rearrange("p j f -> p (j f)")
                    to = out[node0:node0 + p * j, :].rearrange("(p j) f -> p (j f)", j=j)
                    sp.dma_start(to[0:cut], src[0:cut]).then_inc(stored, 16)
                    if cut < p:
                        sp.dma_start(to[cut:p], src[cut:p]).then_inc(stored, 16)
                sp.wait_ge(stored, 16 * (2 + len(late) + (rest_cut < rest_nodes)))

            for i in range(IT):
                if i == 2:
                    sp.dma_start(x_late[:, late_slot[D]:late_slot[REST]],
                                 x[rest0 - 2 * P:rest0, :].rearrange("(n p) f -> p n f", p=P)
                                 ).then_inc(x_late_landed, 16)
                    for r0, r1 in ((0, rest_cut), (rest_cut, rest_nodes)):
                        sp.dma_start(x_late[r0:r1, late_slot[REST]], x[rest0 + r0:rest0 + r1, :]
                                     ).then_inc(x_late_landed, 16)
                load_group(i, i)
            load_x(0)
            for i in range(EARLY):
                sp.wait_ge(group_summed, i + 1)
                load_group(IT + i, i)

            sp.wait_ge(flag_ready, 1)
            general = sp.value_load(flag[0:1, 0:1], min_val=0, max_val=1)
            with sp.If(general > 0):
                sp.wait_ge(group_summed, IT)
                for i in range(EARLY):
                    sp.wait_ge(edges_landed[i], 32)
                step = GEN_TILES * P
                flat = edge_ring[:].rearrange("p s r f -> p (s r) f")
                at = gen_steps * step
                sp.dma_start(flat[0:gen_rest, GEN_TILES], edges[at:n_edges, :]).then_inc(gen_landed, 16)
                sp.dma_start(gen_dst[0:gen_rest, GEN_TILES:GEN_TILES + 1],
                             dst[at:n_edges].rearrange("(e o) -> e o", o=1)).then_inc(gen_landed, 16)
                with sp.Fori(0, gen_steps) as s:
                    sp.wait_ge(gen_tile_used, (blocks + 1) * (1 + GEN_TILES * s))
                    sp.dma_start(flat[:, 0:GEN_TILES].rearrange("p t f -> p (t f)"),
                                 edges[bass.ds(s * step, step), :].rearrange("(p t) f -> p (t f)", t=GEN_TILES)
                                 ).then_inc(gen_landed, 16)
                    sp.dma_start(gen_dst[:, 0:GEN_TILES],
                                 dst[bass.ds(s * step, step)].rearrange("(p t) -> p t", t=GEN_TILES)
                                 ).then_inc(gen_landed, 16)
                with sp.Fori(1, full) as n:
                    load_x(n)
            with sp.Else():
                def iteration(k, i0=0):
                    for i in range(i0, IT):
                        sp.wait_ge(group_summed, IT * k + (i + 1 - IT))
                        load_group(IT * k + i, i)
                        if i == IT - 2 and not same(k, iters - 1):
                            load_x(k)

                iteration(1, EARLY)
                with sp.Fori(2, iters - 1) as k:
                    iteration(k)
                iteration(iters - 1)
                for i in range(tail):
                    g = IT * iters + i
                    sp.wait_ge(group_summed, g - IT + 1)
                    if g < full_grp:
                        load_group(g, i)
                    else:
                        src = edges[g * EDGES_GRP:g * EDGES_GRP + rest_rows * R, :].rearrange("(p r) f -> p (r f)", r=R)
                        to = edge_ring[0:rest_rows, i, 0:R].rearrange("p r f -> p (r f)")
                        cut = rest_rows // 16 * 16
                        sp.dma_start(to[0:cut], src[0:cut]).then_inc(edges_landed[i], 16)
                        if cut < rest_rows:
                            sp.dma_start(to[cut:rest_rows], src[cut:rest_rows]).then_inc(edges_landed[i], 16)
                        sp.dma_start(edge_ring[rest_rows:rest_rows + 1, i, 0:rest_tiles],
                                     edges[n_edges - rest_tiles:n_edges, :].rearrange("(o r) f -> o r f", o=1)
                                     ).then_inc(edges_landed[i], 16)
            store()

        @block.gpsimd
        def _(pool):
            pool.sem_inc(xb_ready, SET)
            nc.gpsimd.iota(row_no[:], [[0, 1]], base=0, channel_multiplier=1,
                           allow_small_or_imprecise_dtypes=True)
            nc.gpsimd.iota(win_row[:], [[0, 1]], base=0, channel_multiplier=WIN,
                           allow_small_or_imprecise_dtypes=True)
            nc.gpsimd.iota(iota[:], [[1, BLOCK]], base=0, channel_multiplier=0,
                           allow_small_or_imprecise_dtypes=True).then_inc(consts_ready, 1)
            nc.gpsimd.memset(ident[:], 0.0).then_inc(consts_ready, 1)
            pool.wait_ge(consts_ready, 2)
            nc.gpsimd.affine_select(out=ident[:], in_=ident[:], compare_op=ALU.not_equal, fill=1.0, base=0,
                                    pattern=[[-1, P]], channel_multiplier=1).then_inc(consts_ready, 1)
            nc.gpsimd.memset(to_window[:], 1.0).then_inc(pool_step, 1)
            pool.wait_ge(pool_step, 1)
            nc.gpsimd.affine_select(out=to_window[:], in_=to_window[:], compare_op=ALU.is_ge, fill=0.0, base=0,
                                    pattern=[[1, P]], channel_multiplier=-WIN).then_inc(pool_step, 1)
            pool.wait_ge(pool_step, 2)
            nc.gpsimd.affine_select(out=to_window[:], in_=to_window[:], compare_op=ALU.is_ge, fill=0.0,
                                    base=WIN - 1, pattern=[[-1, P]], channel_multiplier=WIN).then_inc(consts_ready, 1)
            nc.gpsimd.memset(agg_t[:], 0.0).then_inc(agg_zeroed, 1)

            pool.wait_ge(half_b2_ready, 1)
            pool.wait_ge(x_late_landed, 16 * 4)
            nc.gpsimd.tensor_tensor(xb_late[:, 0:late_slot[REST]], x_late[:, 0:late_slot[REST]],
                                    half_b2[:].unsqueeze(1).broadcast_to([P, late_slot[REST], d]),
                                    ALU.add).then_inc(xb_late_ready, 1)
            nc.gpsimd.tensor_tensor(xb_late[0:rest_nodes, late_slot[REST]], x_late[0:rest_nodes, late_slot[REST]],
                                    half_b2[0:rest_nodes], ALU.add).then_inc(xb_late_ready, 1)
            with pool.Fori(0, full) as n:
                pool.wait_ge(x_landed, 16 * (n + 1))
                pool.wait_ge(y_ready, SET + n)
                nc.gpsimd.tensor_tensor(xb[:], x_sb[:], half_b2[:].unsqueeze(1).broadcast_to([P, J, d]),
                                        ALU.add).then_inc(xb_ready, 1)

            for n in pool_z:
                y_n, moments_n, rstd_n = rows(n, y, y_late), rows(n, mean_var, mean_var_late), rows(n, rstd, rstd_late)
                pool.wait_ge(rstd_ready, n + 1)
                for j in range(pieces[n][2]):
                    last = nc.gpsimd.tensor_scalar(z_rows(n)[:, j], y_n[:, j], moments_n[:, j, 0:1], rstd_n[:, j:j + 1],
                                                   ALU.subtract, ALU.mult)
                last.then_inc(normalized, 1)

        @block.scalar
        def _(act):
            nc.scalar.preload_act_table(ACT.Sqrt)
            act.sem_inc(x_t_ready, SET)
            act.sem_inc(hidden_ready, SET)
            act.sem_inc(late_x_ready, SET)
            loads = [
                (w1_x[:], w1[0:d, :]),
                (w1_a[:], w1[d:2 * d, :]),
                (w1_u[:], w1[2 * d:2 * d + d_glob, :]),
                (u_col[:], u[0:1, :].rearrange("o g -> g o")),
                (b1_col[:], b1.rearrange("(m p) -> p m", p=P)),
                (w2_sb[:], w2.rearrange("(m p) f -> p m f", p=P)),
                (b2_rows[:], b2.rearrange("(o f) -> o f", o=1).broadcast_to([P, d])),
            ]
            assert len(loads) == n_weights
            act.dma_start(base_row[0:1, 1:n_grp + 1],
                          dst.rearrange("(o e) -> o e", o=1)[:, 0:n_edges:EDGES_GRP],
                          allow_slow_non_contiguous=True).then_inc(bases_landed, 16)
            for to, src in loads:
                act.dma_start(to, src, allow_slow_non_contiguous=True).then_inc(weights_landed, 16)

            lt = local_t[:].rearrange("p (g t) -> p t g", t=TILES)
            t0 = 0
            for n, ps in enumerate(turned_to):
                act.wait_ge(local_turned, n + 1)
                t1 = min(t0 + per_bank, TILES)
                last = nc.scalar.copy(lt[:, t0:t1], ps[:, 0:(t1 - t0) * n_grp].rearrange("p (t g) -> p t g", g=n_grp))
                t0 = t1
            last.then_inc(local_t_ready, 1)

            def copy_x_t_late(bank, ns):
                at = 0
                for n in ns:
                    node0, p, j = pieces[n]
                    to = x_t_late[:, node0 - late0:node0 - late0 + p * j]
                    last = nc.scalar.copy(to.rearrange("f (p j) -> f j p", j=j),
                                          bank[:, at:at + p * j].rearrange("f (j p) -> f j p", j=j))
                    at += p * j
                last.then_inc(x_t_late_ready, 1)

            def copy_group(g, i):
                act.wait_ge(group_summed, g + 1)
                if not isinstance(g, int) or g >= 2:
                    act.wait_ge(group_turned, g - 1)
                w = C * WIN if not same(g, full_grp) else WIN
                nc.scalar.copy(sums[0:w, i % 2], sum_ps[i % 2][0:w, 0:d]).then_inc(group_copied, 1)

            def copy_x_t(n):
                act.wait_ge(x_turned, SET + n + 1)
                nc.scalar.copy(x_t[:].rearrange("f (p j) -> f j p", j=J),
                               xt_ps[:].rearrange("f (j p) -> f j p", j=J)).then_inc(x_t_ready, 1)

            def relu(n, m):
                act.wait_ge(hidden_summed, m_chunks * n + m + 1)
                if m == 0:
                    act.wait_ge(out_summed, SET + n)
                nc.scalar.activation(hid_t[:, m].rearrange("h (j p) -> h j p", j=J),
                                     hid_ps[m][:].rearrange("h (p j) -> h j p", j=J), ACT.Relu,
                                     bias=bias[:, m:m + 1]).then_inc(hidden_ready, 1)

            def relu_rest():
                for m in range(m_chunks):
                    act.wait_ge(hidden_summed, m_chunks * REST + m + 1)
                    nc.scalar.activation(hid_t_late[:, m, rest0 - late0:], rest_banks[m], ACT.Relu,
                                         bias=bias[:, m:m + 1]).then_inc(hidden_ready, 1)

            def relu_late(n):
                node0, p, j = pieces[n]
                act.wait_ge(late_x_added, n - full + 1)
                nc.scalar.activation(hid_t_late[:, :, node0 - late0:node0 - late0 + p * j]
                                     .rearrange("h m (j p) -> h m j p", j=j),
                                     late_bank(n).rearrange("h m (p j) -> h m j p", j=j),
                                     ACT.Relu).then_inc(hidden_ready, m_chunks)

            def keep_late_x(k):
                act.wait_ge(late_x_summed, k)
                for m in range(m_chunks):
                    last = nc.scalar.activation(x_hid_late[:, m, bass.ds((k - 1) * x_cols, x_cols)],
                                                hid_ps[m][:, 0:x_cols], ACT.Identity, bias=bias[:, m:m + 1])
                last.then_inc(late_x_ready, 1)

            def root(n):
                _, p, _ = piece(n)
                act.wait_ge(moments_ready, n + 1)
                nc.scalar.activation(rows(n, std, std_late), rows(n, mean_var, mean_var_late)[:, :, 1], ACT.Sqrt,
                                     bias=eps_col[0:p]).then_inc(std_ready, 1)

            for g in range(IT):
                copy_group(g, g)
                if g == 0:
                    act.wait_ge(x_late_turned, 1)
                    copy_x_t_late(hid_ps[1], (A, B))
                    act.wait_ge(x_late_turned, 3)
                    copy_x_t_late(xt_ps, (C_, D, E))
                    copy_x_t_late(hid_ps[0], (REST,))
                if g == 1:
                    act.wait_ge(weights_landed, 16 * n_weights)
                    nc.scalar.mul(half_b2[:], b2_rows[:], 0.5).then_inc(half_b2_ready, 1)
                if g == 2:
                    act.wait_ge(bias_summed, 1)
                    for m in range(m_chunks):
                        last = nc.scalar.activation(bias[:, m:m + 1], out_ps[:, m:m + 1], ACT.Identity,
                                                    bias=b1_col[:, m:m + 1])
                    last.then_inc(bias_ready, 1)
                if g == 4:
                    copy_x_t(0)
            act.wait_ge(bias_ready, 1)
            act.wait_ge(flag_ready, 1)
            general = act.value_load(flag[0:1, 0:1], min_val=0, max_val=1)
            with act.If(general > 0):
                with act.Fori(1, x_steps + 1) as k:
                    keep_late_x(k)

                def mlp(n):
                    if same(n, REST):
                        relu_rest()
                    elif is_late(n):
                        relu_late(n)
                    else:
                        for m in range(m_chunks):
                            relu(n, m)
                    if not is_late(n) and not same(n, LAST):
                        copy_x_t(n + 1)
                    root(n)

                with act.Fori(0, LAST) as n:
                    mlp(n)
                for n in range(LAST, len(pieces)):
                    mlp(n)
            with act.Else():
                def iteration(k, before=True):
                    g = IT * k
                    for i in range(4):
                        copy_group(g + i, i)
                        if i == 0 and before:
                            root(k - 2)
                        if i == 1:
                            relu(k - 1, 0)
                            relu(k - 1, 1)
                    copy_group(g + 4, 4)
                    copy_x_t(k)
                    if not same(k, iters - 2):
                        keep_late_x(k)
                    copy_group(g + 5, 5)

                iteration(1, False)
                with act.Fori(2, iters - 2) as k:
                    iteration(k)
                iteration(iters - 2)
                relu(LAST, 0)
                g = g0
                copy_group(g, 0)
                root(LAST - 1)
                relu(LAST, 1)
                copy_group(g + 1, 1)
                copy_group(g + 2, 2)
                relu_late(A)
                copy_group(g + 3, 3)
                root(LAST)
                copy_group(g + 4, 4)
                relu_late(B)
                copy_group(g + 5, 5)
                root(A)
                g = IT * iters
                copy_group(g, 0)
                copy_group(g + 1, 1)
                root(B)
                relu_late(C_)
                copy_group(g + 2, 2)
                relu_late(D)
                copy_group(full_grp, 3)
                relu_late(E)
                root(C_)
                relu_rest()
                root(D)
                root(E)
                root(REST)

        @block.vector
        def _(dve):
            dve.sem_inc(y_ready, SET)
            dve.sem_inc(normalized, SET)
            nc.vector.memset(dst_rows[64:P, 0, rest_edges:], n_nodes - 1)
            nc.vector.memset(dst_rows[64:P, 1:C], n_nodes - 1).then_inc(pad_set, 1)
            nc.vector.memset(base_row[0:1, 0:1], 0)
            nc.vector.memset(base_row[0:1, n_grp + 1:], 0)
            nc.vector.memset(eps_col[:], EPS).then_inc(pad_set, 1)
            dve.wait_ge(consts_ready, 1)
            nc.vector.tensor_scalar(least_base[:], row_no[:], BLOCK / IT, None, ALU.mult)
            for n, (g, least) in enumerate(late_groups):
                last = nc.vector.tensor_scalar(late_base[:, n:n + 1], row_no[:], g - 0.5, float(least),
                                               ALU.is_gt, ALU.mult)
            last.then_inc(pad_set, 1)
            dve.wait_ge(pad_set, 3)
            for n in range(len(late_groups)):
                nc.vector.tensor_tensor(least_base[:], least_base[:], late_base[:, n:n + 1],
                                        ALU.max).then_inc(pad_set, 1)
                dve.wait_ge(pad_set, 4 + n)
            dve.wait_ge(bases_landed, 16)
            nc.vector.tensor_scalar(bases[0:1, :].rearrange("o (k i) -> o k i", i=BASE_PITCH)[:, :, 0:IT],
                                    base_row[0:1, :].rearrange("o (k i) -> o k i", i=IT),
                                    float(n_nodes - 1), 0.0, ALU.min, ALU.max).then_inc(prep, 1)
            dve.wait_ge(dst_landed, 48)
            nc.vector.tensor_copy(base_f[0:n_grp], dst_rows[0:n_grp, :, 0]).then_inc(prep, 1)
            dve.wait_ge(prep, PREP_BASE_F)
            nc.vector.tensor_scalar(rel[0:n_grp], base_f[0:n_grp], base_f[0:n_grp, 0:1], None,
                                    ALU.subtract).then_inc(rel_ready, 1)
            nc.vector.tensor_tensor(local_rows[0:n_grp], dst_rows[0:n_grp],
                                    base_f[0:n_grp].unsqueeze(2).broadcast_to([n_grp, C, EDGES_WIN]),
                                    ALU.subtract).then_inc(prep, 1)
            dve.wait_ge(rel_turned, 1)
            nc.vector.tensor_scalar(rel_t[:, 0:n_grp], out_ps[0:C, rel_at], win_row[:], None,
                                    ALU.subtract).then_inc(rel_t_ready, 1)
            dve.wait_ge(rel_spread, 1)
            nc.vector.tensor_scalar(rel_cols[:], out_ps[:, spread_at], row_no[:], None,
                                    ALU.add).then_inc(rel_cols_ready, 1)
            dve.wait_ge(prep, PREP_LOCAL)

            def make_onehot(g, slot):
                loc = local_t[:, bass.ds(g * TILES, TILES)].unsqueeze(2).broadcast_to([P, TILES, WIN])
                cols = iota[:, 0:WIN].unsqueeze(1).broadcast_to([P, TILES, WIN])
                nc.vector.tensor_tensor(onehot[:, slot], cols, loc, ALU.is_equal).then_inc(onehot_ready, 1)

            def next_onehot(g, i):
                if not isinstance(g, int) or g + LEAD >= ONEHOTS:
                    dve.wait_ge(group_summed, g + LEAD - ONEHOTS + 1)
                make_onehot(g + LEAD, (i + LEAD) % ONEHOTS)

            def load_bases(k, n=IT):
                _, vals = nc.values_load_multi_w_load_instructions(
                    bases[0:1, bass.ds(k * BASE_PITCH, n)], engines=[mybir.EngineType.DVE],
                    min_val=0, max_val=n_nodes - 1,
                    skip_runtime_bounds_check_because="bases were clamped to the nodes on the chip")
                return vals

            def make_place(g, i):
                nc.vector.tensor_scalar(place[:, i % PLACES], iota[:, 0:SPAN], rel_cols[:, bass.ds(g, 1)], None,
                                        ALU.is_equal).then_inc(place_ready, 1)

            def add_group(g, i, base):
                dve.wait_ge(group_turned, g + 1)
                dve.wait_ge(group_added, g)
                to = agg_t[:, bass.ds(base, SPAN)]
                nc.vector.tensor_tensor(to, to, turn_ps[i % 2][:, 0:SPAN], ALU.add).then_inc(group_added, 1)

            def add_late_x(n):
                node0, p, j = pieces[n]
                dve.wait_ge(late_x_ready, SET + x_steps)
                dve.wait_ge(hidden_summed, m_chunks * (n + 1))
                nc.vector.tensor_tensor(late_bank(n), late_bank(n),
                                        x_hid_late[:, :, node0 - late0:node0 - late0 + p * j],
                                        ALU.add).then_inc(late_x_added, 1)

            def norm_step(n, step):
                _, p, j = piece(n)
                y_n, stats_n = rows(n, y, y_late), rows(n, stats, stats_late)
                moments_n = rows(n, mean_var, mean_var_late)
                std_n, rstd_n, z_n = rows(n, std, std_late), rows(n, rstd, rstd_late), z_rows(n)
                if step == 0:
                    dve.wait_ge(out_summed, SET + n + 1)
                    if is_late(n):
                        dve.wait_ge(xb_late_ready, 2)
                    else:
                        dve.wait_ge(xb_ready, SET + n + 1)
                        dve.wait_ge(normalized, SET + n)
                    nc.vector.scalar_tensor_tensor(
                        out=y_n.rearrange("p j f -> p (j f)"), in0=rows(n, xb, xb_late).rearrange("p j f -> p (j f)"),
                        scalar=2.0, in1=out_bank(n)[0:p, 0:j * d], op0=ALU.mult, op1=ALU.add).then_inc(y_ready, 1)
                elif step == 1:
                    dve.wait_ge(y_ready, SET + n + 1)
                    for jj in range(j):
                        last = nc.vector.bn_stats(stats_n[:, jj], y_n[:, jj])
                    last.then_inc(stats_ready, 1)
                elif step == 2:
                    dve.wait_ge(flag_ready, 1)
                    dve.wait_ge(stats_ready, n + 1)
                    for jj in range(j):
                        last = nc.vector.bn_aggr(moments_n[:, jj], stats_n[:, jj])
                    last.then_inc(moments_ready, 1)
                elif step == 3:
                    dve.wait_ge(std_ready, n + 1)
                    nc.vector.reciprocal(rstd_n, std_n).then_inc(rstd_ready, 1)
                elif isinstance(n, int) and n in pool_z:
                    pass
                elif step == 4:
                    dve.wait_ge(rstd_ready, n + 1)
                    for jj in range(j):
                        last = nc.vector.tensor_scalar(z_n[:, jj], y_n[:, jj], moments_n[:, jj, 0:1],
                                                       rstd_n[:, jj:jj + 1], ALU.subtract, ALU.mult)
                    last.then_inc(end_normalized if is_late(n) else normalized, 1)

            def moments(n):
                for step in range(3):
                    norm_step(n, step)

            def normalize(n):
                for step in (3, 4):
                    norm_step(n, step)

            dve.wait_ge(local_t_ready, 1)
            for g in range(LEAD):
                make_onehot(g, g)
            dve.wait_ge(rel_cols_ready, 1)
            make_place(0, 0)
            dve.wait_ge(agg_zeroed, 1)
            base0 = load_bases(0)

            def check(step):
                if step == 0:
                    nc.vector.tensor_reduce(extreme[0:n_grp, 0], local_rows[0:n_grp], AX_X, ALU.max)
                elif step == 1:
                    nc.vector.tensor_reduce(extreme[0:n_grp, 1], local_rows[0:n_grp], AX_X, ALU.min).then_inc(prep, 1)
                elif step == 2:
                    dve.wait_ge(prep, PREP_EXTREME)
                    nc.vector.tensor_scalar(viol[0:n_grp, 0], extreme[0:n_grp, 0], float(WIN - 1), None, ALU.subtract)
                    nc.vector.tensor_scalar(viol[0:n_grp, 1], extreme[0:n_grp, 1], -1.0, None, ALU.mult)
                    nc.vector.tensor_scalar(viol[0:n_grp, 2], base_f[0:n_grp], -1.0, least_base[0:n_grp],
                                            ALU.mult, ALU.add)
                    nc.vector.tensor_scalar(viol[0:n_grp, 3], base_f[0:n_grp], float(n_nodes - 1), None,
                                            ALU.subtract)
                    nc.vector.tensor_scalar(viol[0:n_grp, 4], rel[0:n_grp], float(SPAN - WIN), None, ALU.subtract)
                    nc.vector.tensor_scalar(viol[0:n_grp, 5], rel[0:n_grp], -1.0, None, ALU.mult).then_inc(prep, 1)
                    dve.wait_ge(prep, PREP_VIOL)
                    nc.vector.tensor_reduce(worst[0:n_grp], viol[0:n_grp].rearrange("g v c -> g (v c)"), AX_X,
                                            ALU.max).then_inc(worst_ready, 1)
                elif step == 4:
                    dve.wait_ge(worst_turned, 1)
                    nc.vector.tensor_reduce(worst_row[0:1], out_ps[0:1, worst_at], AX_X,
                                            ALU.max).then_inc(prep, 1)
                    dve.wait_ge(prep, PREP_WORST_ROW)
                    nc.vector.tensor_scalar(flag[0:1], worst_row[0:1], 0.0, None, ALU.is_gt).then_inc(flag_ready, 1)

            for g in range(IT):
                next_onehot(g, g)
                make_place(g + 1, g + 1)
                if g > 0:
                    add_group(g - 1, g - 1, base0[g])
                check(g)

            dve.wait_ge(flag_ready, 1)
            general = dve.value_load(flag[0:1, 0:1], min_val=0, max_val=1)
            with dve.If(general > 0):
                dve.wait_ge(group_added, IT - 1)
                nc.vector.memset(agg_t[:], 0.0).then_inc(gen_zeroed, 1)
                dve.wait_ge(gen_zeroed, 1)

                def gen_match(tiles, rows, t0, rel_count, tiles_before, adds_before):
                    for t in range(tiles):
                        dve.wait_ge(gen_tile_used, tiles_before + t - 1)
                        nc.vector.tensor_scalar(gen_onehot[0:rows, t % 2], iota[0:rows],
                                                gen_rel[0:rows, t0 + t:t0 + t + 1], None, ALU.is_equal).then_inc(gen_onehot_ready, 1)
                    dve.wait_ge(gen_tile_used, tiles_before + tiles)
                    nc.vector.tensor_scalar(gen_rel[0:rows, t0:t0 + tiles], gen_rel[0:rows, t0:t0 + tiles],
                                            -float(BLOCK), None, ALU.add).then_inc(gen_rel_ready, 1)
                    dve.wait_ge(gen_rel_ready, rel_count)
                    dve.wait_ge(gen_added, adds_before)

                def gen_add(nb):
                    at = agg_t[:, bass.ds(nb * BLOCK, BLOCK)]
                    nc.vector.tensor_tensor(at, at, sum_ps[0][:, :], ALU.add).then_inc(gen_added, 1)

                dve.wait_ge(gen_landed, 32)
                nc.vector.tensor_copy(gen_rel[0:gen_rest, GEN_TILES:], gen_dst[0:gen_rest, GEN_TILES:]
                                      ).then_inc(gen_rel_ready, 1)
                dve.wait_ge(gen_rel_ready, 1)
                for nb in range(blocks + 1):
                    nc.vector.tensor_scalar(gen_onehot[0:gen_rest, 0], iota[0:gen_rest],
                                            gen_rel[0:gen_rest, GEN_TILES:], None,
                                            ALU.is_equal).then_inc(gen_onehot_ready, 1)
                    dve.wait_ge(gen_tile_used, nb + 1)
                    nc.vector.tensor_scalar(gen_rel[0:gen_rest, GEN_TILES:], gen_rel[0:gen_rest, GEN_TILES:],
                                            -float(BLOCK), None, ALU.add).then_inc(gen_rel_ready, 1)
                    dve.wait_ge(gen_rel_ready, nb + 2)
                    gen_add(nb)
                nbs = blocks + 1
                with dve.Fori(0, gen_steps) as s:
                    dve.wait_ge(gen_landed, 32 * s + 64)
                    nc.vector.tensor_copy(gen_rel[:, 0:GEN_TILES], gen_dst[:, 0:GEN_TILES]).then_inc(gen_rel_ready, 1)
                    with dve.Fori(0, nbs) as nb:
                        n = nbs * s + nb
                        dve.wait_ge(gen_rel_ready, (nbs + 1) * (s + 1) + 1 + nb)
                        gen_match(GEN_TILES, P, 0, (nbs + 1) * (s + 1) + 2 + nb, nbs + GEN_TILES * n, nbs + n)
                        gen_add(nb)
                with dve.Fori(0, LAST) as n:
                    moments(n)
                    normalize(n)
                for n in range(LAST, len(pieces)):
                    if is_late(n) and n != REST:
                        add_late_x(n)
                    moments(n)
                    normalize(n)
            with dve.Else():
                def group(g, i, bases_before):
                    if not isinstance(g, int) or g + LEAD < n_grp:
                        next_onehot(g, i)
                    if not same(g, full_grp):
                        make_place(g + 1, i + 1)
                    add_group(g - 1, (i - 1) % IT, bases_before[i])

                def iteration(k, before=True):
                    base = load_bases(k)
                    for i in range(IT):
                        group(IT * k + i, i, base)
                        if i == 1 and before:
                            normalize(k - 2)
                        if i == 4:
                            moments(k - 1)

                iteration(1, False)
                with dve.Fori(2, iters - 1) as k:
                    iteration(k)
                base = load_bases(iters - 1)
                for i in range(IT):
                    group(g0 + i, i, base)
                    if i == 1:
                        normalize(LAST - 1)
                    if i == 2:
                        add_late_x(A)
                    if i == 3:
                        moments(LAST)
                        add_late_x(B)
                    if i == 4:
                        normalize(LAST)
                    if i == 5:
                        moments(A)
                g = IT * iters
                base = load_bases(iters, tail + 1)
                group(g, 0, base)
                normalize(A)
                moments(B)
                group(g + 1, 1, base)
                normalize(B)
                add_late_x(C_)
                add_late_x(D)
                group(g + 2, 2, base)
                group(full_grp, 3, base)
                norm_step(C_, 0)
                norm_step(C_, 1)
                add_group(full_grp, 3, base[tail])
                add_late_x(E)
                norm_step(C_, 2)
                moments(D)
                normalize(C_)
                normalize(D)
                for step in range(5):
                    norm_step(E, step)
                    norm_step(REST, step)

        @block.tensor
        def _(pe):
            pe.sem_inc(x_turned, SET)
            pe.sem_inc(out_summed, SET)
            pe.wait_ge(consts_ready, 4)
            pe.wait_ge(rel_ready, 1)
            nc.tensor.transpose(out_ps[0:C, rel_at], rel[0:n_grp, :], ident[0:n_grp, 0:n_grp]).then_inc(rel_turned, 1)
            pe.wait_ge(rel_t_ready, 1)
            nc.tensor.matmul(out_ps[:, spread_at], to_window[:], rel_t[:, 0:n_grp], start=True,
                             stop=True).then_inc(rel_spread, 1)
            pe.wait_ge(prep, PREP_LOCAL)
            for t in range(TILES):
                c, r = divmod(t, R)
                ps, col = turned_to[t // per_bank], t % per_bank
                last = nc.tensor.transpose(ps[:, col * n_grp:(col + 1) * n_grp], local_rows[0:n_grp, c, r::R],
                                           ident[0:n_grp, 0:n_grp])
                if col == per_bank - 1 or t == TILES - 1:
                    last.then_inc(local_turned, 1)

            def sum_group(g, i, rounds):
                pe.wait_ge(edges_landed[i], 16 * rounds)
                pe.wait_ge(onehot_ready, g + 1)
                if not isinstance(g, int) or g >= 2:
                    pe.wait_ge(group_copied, g - 1)
                for r in range(R):
                    for c in range(C if not same(g, full_grp) else 1):
                        p = P if not same(g, full_grp) else rest_rows + (r < rest_tiles)
                        last = nc.tensor.matmul(sum_ps[i % 2][c * WIN:(c + 1) * WIN, 0:d],
                                                onehot[0:p, i % ONEHOTS, c * R + r], edge_ring[0:p, i, c * R + r],
                                                start=(r == 0), stop=(r == R - 1))
                last.then_inc(group_summed, 1)

            def turn_group(g, i):
                pe.wait_ge(group_copied, g + 1)
                pe.wait_ge(place_ready, g + 1)
                if not isinstance(g, int) or g >= 2:
                    pe.wait_ge(group_added, g - 1)
                w = C * WIN if not same(g, full_grp) else WIN
                nc.tensor.matmul(turn_ps[i % 2][:, 0:SPAN], sums[0:w, i % 2], place[0:w, i % PLACES],
                                 start=True, stop=True).then_inc(group_turned, 1)

            def turn_x(n):
                pe.wait_ge(x_landed, 16 * (n + 1))
                pe.wait_ge(x_t_ready, SET + n)
                for j in range(J):
                    last = nc.tensor.transpose(xt_ps[:, j * P:(j + 1) * P], x_sb[:, j], ident[:])
                last.then_inc(x_turned, 1)

            def turn_x_late(bank, ns):
                at = 0
                for n in ns:
                    _, p, j = pieces[n]
                    for jj in range(j):
                        last = nc.tensor.transpose(bank[:, at:at + p], x_late[0:p, late_slot[n] + jj], ident[0:p, 0:p])
                        at += p
                last.then_inc(x_late_turned, 1)

            def sum_late_x(k, after_block=True):
                if after_block:
                    pe.wait_ge(hidden_ready, SET + m_chunks * k)
                pe.wait_ge(late_x_ready, SET + (k - 1))
                for m in range(m_chunks):
                    last = nc.tensor.matmul(hid_ps[m][:, 0:x_cols], w1_x[:, m * P:(m + 1) * P],
                                            x_t_late[:, bass.ds((k - 1) * x_cols, x_cols)], start=True, stop=True)
                last.then_inc(late_x_summed, 1)

            def sum_hidden(n, chunks, complete=None):
                sum_hidden_x(n, chunks)
                sum_hidden_a(n, chunks, complete)

            def sum_hidden_x(n, chunks):
                pe.wait_ge(x_t_ready, SET + n + 1)
                pe.wait_ge(late_x_ready, SET + (min(n, x_steps) if isinstance(n, int) else n))
                pe.wait_ge(hidden_ready, SET + m_chunks * n)
                for m in chunks:
                    nc.tensor.matmul(hid_ps[m][:], w1_x[:, m * P:(m + 1) * P], x_t[:], start=True, stop=False)

            def sum_hidden_a(n, chunks, complete):
                if complete is not None:
                    pe.wait_ge(group_added, complete)
                for m in chunks:
                    nc.tensor.matmul(hid_ps[m][:], w1_a[:, m * P:(m + 1) * P], agg_t[:, bass.ds(n * BLOCK, BLOCK)],
                                     start=False, stop=True).then_inc(hidden_summed, 1)

            def sum_hidden_late(n, complete=None):
                node0, p, j = pieces[n]
                pe.wait_ge(hidden_ready, SET + m_chunks * max(n - 1, full))
                if complete is not None:
                    pe.wait_ge(group_added, complete)
                for m in range(m_chunks):
                    nc.tensor.matmul(late_bank(n)[:, m], w1_a[:, m * P:(m + 1) * P], agg_t[:, node0:node0 + p * j],
                                     start=True, stop=True).then_inc(hidden_summed, 1)

            def sum_hidden_rest(complete=None):
                for m in range(m_chunks):
                    nc.tensor.matmul(rest_banks[m], w1_x[:, m * P:(m + 1) * P],
                                     x_t_late[:, rest0 - late0:], start=True, stop=False)
                if complete is not None:
                    pe.wait_ge(group_added, complete)
                for m in range(m_chunks):
                    nc.tensor.matmul(rest_banks[m], w1_a[:, m * P:(m + 1) * P], agg_t[:, rest0:n_nodes],
                                     start=False, stop=True).then_inc(hidden_summed, 1)

            def sum_out(n, rows_j=None):
                node0, p, j = piece(n)
                rows_j = range(j) if rows_j is None else rows_j
                if 0 in rows_j:
                    pe.wait_ge(hidden_ready, SET + m_chunks * (n + 1))
                    if not same(n, A):
                        pe.wait_ge(y_ready, SET + n - is_late(n))
                hidden_t, at = (hid_t_late, node0 - late0) if is_late(n) else (hid_t, 0)
                for jj in rows_j:
                    for m in range(m_chunks):
                        last = nc.tensor.matmul(out_bank(n)[0:p, jj * d:(jj + 1) * d],
                                                hidden_t[:, m, at + jj * p:at + (jj + 1) * p],
                                                w2_sb[:, m], start=(m == 0), stop=(m == m_chunks - 1))
                if j - 1 in rows_j:
                    last.then_inc(out_summed, 1)

            pe.wait_ge(local_t_ready, 1)
            for g in range(IT):
                sum_group(g, g, 1)
                if g == 0:
                    pe.wait_ge(x_late_landed, 16 * 4)
                    turn_x_late(hid_ps[1], (A, B))
                    turn_x_late(xt_ps, (C_, D, E))
                    turn_x_late(hid_ps[0], (REST,))
                if g > 0:
                    turn_group(g - 1, g - 1)
                if g == 2:
                    pe.wait_ge(rel_cols_ready, 1)
                    pe.wait_ge(weights_landed, 16 * n_weights)
                    for m in range(m_chunks):
                        last = nc.tensor.matmul(out_ps[:, m:m + 1], w1_u[:, m * P:(m + 1) * P], u_col[:],
                                                start=True, stop=True)
                    last.then_inc(bias_summed, 1)
                if g == 3:
                    pe.wait_ge(bias_ready, 1)
                    pe.wait_ge(worst_ready, 1)
                    nc.tensor.transpose(out_ps[0:1, worst_at], worst[0:n_grp, 0:1],
                                        ident[0:n_grp, 0:n_grp]).then_inc(worst_turned, 1)
                if g == 4:
                    pe.wait_ge(x_t_late_ready, 3)
                    turn_x(0)
            pe.wait_ge(flag_ready, 1)
            general = pe.value_load(flag[0:1, 0:1], min_val=0, max_val=1)
            with pe.If(general > 0):
                flat = edge_ring[:].rearrange("p s r f -> p (s r) f")
                nbs = blocks + 1
                pe.wait_ge(group_copied, IT)
                pe.wait_ge(gen_zeroed, 1)
                pe.wait_ge(gen_landed, 32)
                for nb in range(nbs):
                    pe.wait_ge(gen_onehot_ready, nb + 1)
                    pe.wait_ge(gen_added, nb)
                    nc.tensor.matmul(sum_ps[0][:, :], flat[0:gen_rest, GEN_TILES], gen_onehot[0:gen_rest, 0],
                                     start=True, stop=True).then_inc(gen_tile_used, 1)
                with pe.Fori(0, gen_steps) as s:
                    with pe.Fori(0, nbs) as nb:
                        n = nbs * s + nb
                        pe.wait_ge(gen_landed, 32 * s + 64)
                        pe.wait_ge(gen_added, nbs + n)
                        for t in range(GEN_TILES):
                            pe.wait_ge(gen_onehot_ready, nbs + GEN_TILES * n + (t + 1))
                            nc.tensor.matmul(sum_ps[0][:, :], flat[:, t], gen_onehot[:, t % 2],
                                             start=(t == 0), stop=(t == GEN_TILES - 1)).then_inc(gen_tile_used, 1)
                pe.wait_ge(gen_added, nbs * (1 + gen_steps))

                with pe.Fori(1, x_steps + 1) as k:
                    sum_late_x(k, False)
                pe.wait_ge(late_x_ready, SET + x_steps)

                def mlp(n):
                    if same(n, REST):
                        sum_hidden_rest()
                    elif is_late(n):
                        sum_hidden_late(n)
                    else:
                        for m in range(m_chunks):
                            sum_hidden(n, [m])
                    sum_out(n)
                    if not is_late(n) and not same(n, LAST):
                        turn_x(n + 1)

                with pe.Fori(0, LAST) as n:
                    mlp(n)
                for n in range(LAST, len(pieces)):
                    mlp(n)
            with pe.Else():
                def group(g, i, rounds):
                    sum_group(g, i, rounds)
                    turn_group(g - 1, (i - 1) % IT)

                def hidden(n):
                    sum_hidden_late(n, complete_at[n])

                def iteration(k):
                    n, g = k - 1, IT * k
                    for i in range(IT):
                        group(g + i, i, k + 1)
                        if i == 0:
                            sum_hidden_x(n, range(m_chunks))
                        if i == 1:
                            sum_hidden_a(n, range(m_chunks), g)
                        if i == 2:
                            sum_out(n, [0, 1])
                        if i == 3:
                            sum_out(n, [2, 3])
                        if i == 4:
                            turn_x(n + 1)
                            if not same(k, iters - 2):
                                sum_late_x(k)

                with pe.Fori(1, iters - 2) as k:
                    iteration(k)
                iteration(iters - 2)
                sum_hidden(LAST, [0], LAST_COMPLETE)
                for i in range(IT):
                    sum_group(g0 + i, i, iters)
                    if i == 4:
                        hidden(B)
                    turn_group(g0 + i - 1, (i - 1) % IT)
                    if i == 0:
                        sum_hidden(LAST, [1])
                    if i == 1:
                        sum_out(LAST)
                    if i == 2:
                        hidden(A)
                    if i == 4:
                        sum_out(A)
                    if i == 5:
                        sum_out(B)
                g, rounds = IT * iters, iters + 1
                group(g, 0, rounds)
                group(g + 1, 1, rounds)
                hidden(C_)
                sum_group(g + 2, 2, rounds)
                hidden(D)
                turn_group(g + 1, 1)
                group(full_grp, 3, iters + 2 + (rest_rows % 16 > 0))
                sum_out(C_)
                turn_group(full_grp, 3)
                hidden(E)
                sum_out(D)
                sum_hidden_rest(complete_at[REST])
                sum_out(E)
                sum_out(REST)


_INS = ["x", "dst", "edge_attr_128", "L0_gnn_u", "L0_gnn_W1", "L0_gnn_b1", "L0_gnn_W2", "L0_gnn_b2"]


def kernel(**inputs):
    import numpy as _np
    import concourse.bacc as _bacc
    from concourse import mybir as _mybir
    from concourse.bass_utils import run_bass_kernel_spmd as _run

    nc = _bacc.Bacc("TRN2", target_bir_lowering=False, num_devices=1)
    arrays, args = {}, []
    for name in _INS:
        a = _np.ascontiguousarray(inputs[name])
        arrays[f"in_{name}_dram"] = a
        args.append(nc.dram_tensor(f"in_{name}_dram", a.shape, _mybir.dt.from_np(a.dtype), kind="ExternalInput").ap())
    shape = _np.shape(inputs["x"])
    args.append(nc.dram_tensor("out_0_dram", shape, _mybir.dt.float32, kind="ExternalOutput").ap())
    gnn_resnorm_kernel(nc, *args)
    r = _run(nc, [arrays], core_ids=[0])
    return r.results[0]["out_0_dram"]
```
